# Optimizing a Trainium2 kernel written in Bass

```python
import numpy as np
import jax
import jax.numpy as jnp

def _softmax(x, axis=-1):
    return jax.nn.softmax(x, axis=axis)

def _gelu(x):
    return jax.nn.gelu(x, approximate=True)

def _silu(x):
    return jax.nn.silu(x)

def _sigmoid(x):
    return jax.nn.sigmoid(x)

def _layernorm(x, axis=-1, eps=1e-05):
    m = jnp.mean(x, axis=axis, keepdims=True)
    v = jnp.var(x, axis=axis, keepdims=True)
    return (x - m) / jnp.sqrt(v + eps)

def _scatter_add(tgt, idx, src, axis=0):
    return tgt.at[idx].add(src)

def _segment_sum(src, seg, n):
    return jax.ops.segment_sum(src, seg, n)
kernel_name = 'mk_gnn_preln_d4_gnn_r32_900d8f'

def setup_inputs(seed: int=0):
    np.random.seed(seed)
    _w = jnp.asarray

    def _rec_inputs():
        import jax
        import jax.numpy as jnp
        _gk = jax.random.key(seed)
        x = -0.0002928 + 1 * jax.random.normal(jax.random.fold_in(_gk, 1), (256, 512), jnp.float32)
        _s = jax.random.randint(jax.random.fold_in(_gk, 2), (2048,), 0, 256, jnp.int32)
        _d = jax.random.randint(jax.random.fold_in(_gk, 3), (2048,), 0, 256, jnp.int32)
        _loop = jnp.arange(256, dtype=jnp.int32)
        src = jnp.concatenate([_s, _d, _loop])
        dst = jnp.concatenate([_d, _s, _loop])
        _o = jnp.argsort(dst, stable=True)
        src = src[_o]
        dst = dst[_o]
        edge_weight = jax.random.uniform(jax.random.fold_in(_gk, 13), (4352,), jnp.float32, 0.0, 0.999994)
        return (x, src, dst, edge_weight)
    x, src, dst, edge_weight = _rec_inputs()

    def _L0_gnn_setup():
        import jax, jax.numpy as jnp
        import numpy as np
        N = 256
        D = 512
        E = 8192
        STEPS = 3
        key = jax.random.key(seed)
        k1, k2, k3 = jax.random.split(key, 3)
        x = jax.random.normal(k1, (N, D), dtype=jnp.float32)
        edge_index = jax.random.randint(k2, (2, E), 0, N, dtype=jnp.int32)
        W = jax.random.normal(k3, (D, D), dtype=jnp.float32) / np.sqrt(D)
        b = jnp.zeros((D,), dtype=jnp.float32)
        diffusion_weights = jnp.ones((STEPS + 1,), dtype=jnp.float32) / (STEPS + 1)
        return {'x': x, 'edge_index': edge_index, 'W': W, 'b': b, 'diffusion_weights': diffusion_weights}
    _L0_gnn_all = _L0_gnn_setup()
    _L0_gnn_in = {k: v for k, v in _L0_gnn_all.items() if k in ('W', 'b', 'diffusion_weights')}
    del _L0_gnn_all

    def _L1_gnn_setup():
        import jax, jax.numpy as jnp
        import numpy as np
        N, E, H, D_IN, D_PRIME = (50000, 25000, 8, 512, 64)

        def _segment_softmax(scores, seg, num_segments):
            smax = jax.ops.segment_max(scores, seg, num_segments=num_segments)
            ex = jnp.exp(scores - smax[seg])
            denom = jax.ops.segment_sum(ex, seg, num_segments=num_segments)
            return ex / denom[seg]
        key = jax.random.key(seed)
        ks = jax.random.split(key, 6)
        x = jax.random.normal(ks[0], (N, D_IN), dtype=jnp.float32)
        edge_index = jax.random.randint(ks[1], (2, E), 0, N)
        Ws = jax.random.normal(ks[2], (H, D_IN, D_PRIME), dtype=jnp.float32) * 0.05
        Wb = jax.random.normal(ks[3], (H, D_PRIME), dtype=jnp.float32) * 0.05
        a_w = jax.random.normal(ks[4], (H, 2 * D_PRIME), dtype=jnp.float32) * 0.05
        a_b = jax.random.normal(ks[5], (H,), dtype=jnp.float32) * 0.05
        return dict(x=x, edge_index=edge_index, Ws=Ws, Wb=Wb, a_w=a_w, a_b=a_b)
    _L1_gnn_all = _L1_gnn_setup()
    _L1_gnn_in = {k: v for k, v in _L1_gnn_all.items() if k in ('Ws', 'Wb', 'a_w', 'a_b')}
    del _L1_gnn_all

    def _L2_gnn_setup():
        import jax, jax.numpy as jnp
        import numpy as np
        N_NODES = 50000
        N_EDGES = 25000
        D_IN = 512
        D_OUT = 512
        EPS = 1e-05
        key = jax.random.key(seed)
        k1, k2, k3, k4, k5 = jax.random.split(key, 5)
        x = jax.random.normal(k1, (N_NODES, D_IN), dtype=jnp.float32)
        edge_index = jax.random.randint(k2, (2, N_EDGES), 0, N_NODES, dtype=jnp.int64)
        s = 1.0 / np.sqrt(D_IN)
        W_l = jax.random.uniform(k3, (D_OUT, D_IN), jnp.float32, -s, s)
        b_l = jnp.zeros((D_OUT,), jnp.float32)
        W_r = jax.random.uniform(k4, (D_OUT, D_IN), jnp.float32, -s, s)
        gamma = jnp.ones((D_OUT,), jnp.float32)
        beta = jnp.zeros((D_OUT,), jnp.float32)
        return {'x': x, 'edge_index': edge_index, 'W_l': W_l, 'b_l': b_l, 'W_r': W_r, 'gamma': gamma, 'beta': beta}
    _L2_gnn_all = _L2_gnn_setup()
    _L2_gnn_in = {k: v for k, v in _L2_gnn_all.items() if k in ('W_l', 'b_l', 'W_r', 'gamma', 'beta')}
    del _L2_gnn_all

    def _L3_gnn_setup():
        import jax, jax.numpy as jnp
        import numpy as np
        N_NODES = 625
        N_EDGES = 5000
        N_IN = 512
        N_OUT = 512
        key = jax.random.key(seed)
        k1, k2, k3, k4, k5 = jax.random.split(key, 5)
        x = jax.random.normal(k1, (N_NODES, N_IN), dtype=jnp.float32)
        vals = jax.random.uniform(k2, (N_EDGES,), dtype=jnp.float32)
        bound = 1.0 / np.sqrt(N_IN)
        weight = jax.random.uniform(k3, (N_OUT, N_IN), minval=-bound, maxval=bound, dtype=jnp.float32)
        row = jax.random.randint(k4, (N_EDGES,), 0, N_NODES, dtype=jnp.int32)
        col = jax.random.randint(k5, (N_EDGES,), 0, N_NODES, dtype=jnp.int32)
        return {'x': x, 'vals': vals, 'weight': weight, 'row': row, 'col': col}
    _L3_gnn_all = _L3_gnn_setup()
    _L3_gnn_in = {k: v for k, v in _L3_gnn_all.items() if k in ('weight',)}
    del _L3_gnn_all
    return {'x': x, 'src': src, 'dst': dst, 'edge_weight': edge_weight, 'L0_gnn_W': _L0_gnn_in['W'], 'L0_gnn_b': _L0_gnn_in['b'], 'L0_gnn_diffusion_weights': _L0_gnn_in['diffusion_weights'], 'L1_gnn_Ws': _L1_gnn_in['Ws'], 'L1_gnn_Wb': _L1_gnn_in['Wb'], 'L1_gnn_a_w': _L1_gnn_in['a_w'], 'L1_gnn_a_b': _L1_gnn_in['a_b'], 'L2_gnn_W_l': _L2_gnn_in['W_l'], 'L2_gnn_b_l': _L2_gnn_in['b_l'], 'L2_gnn_W_r': _L2_gnn_in['W_r'], 'L2_gnn_gamma': _L2_gnn_in['gamma'], 'L2_gnn_beta': _L2_gnn_in['beta'], 'L3_gnn_weight': _L3_gnn_in['weight']}

def reference(x, src, dst, edge_weight, L0_gnn_W, L0_gnn_b, L0_gnn_diffusion_weights, L1_gnn_Ws, L1_gnn_Wb, L1_gnn_a_w, L1_gnn_a_b, L2_gnn_W_l, L2_gnn_b_l, L2_gnn_W_r, L2_gnn_gamma, L2_gnn_beta, L3_gnn_weight):
    import jax
    import jax.numpy as jnp

    def _L0_gnn_ref(x, edge_index, W, b, diffusion_weights):
        import jax, jax.numpy as jnp
        import numpy as np
        N = 256
        D = 512
        E = 8192
        STEPS = 3
        h = x @ W + b
        row, col = (edge_index[0], edge_index[1])
        adj = jnp.zeros((N, N), dtype=h.dtype)
        adj = adj.at[row, col].set(1.0)
        adj = adj.at[col, row].set(1.0)
        adj = adj + jnp.eye(N, dtype=h.dtype)
        row_sum = adj.sum(axis=1, keepdims=True)
        adj = adj / jnp.maximum(row_sum, 1.0)
        out = diffusion_weights[0] * h
        cur = h
        for i in range(STEPS):
            cur = adj @ cur
            out = out + diffusion_weights[i + 1] * cur
        return jax.nn.relu(out)

    def _L1_gnn_ref(x, edge_index, Ws, Wb, a_w, a_b):
        import jax, jax.numpy as jnp
        import numpy as np
        N, E, H, D_IN, D_PRIME = (50000, 25000, 8, 512, 64)

        def _segment_softmax(scores, seg, num_segments):
            smax = jax.ops.segment_max(scores, seg, num_segments=num_segments)
            ex = jnp.exp(scores - smax[seg])
            denom = jax.ops.segment_sum(ex, seg, num_segments=num_segments)
            return ex / denom[seg]
        v_src, v_tgt = (edge_index[0], edge_index[1])
        n = x.shape[0]
        outs = []
        for h in range(Ws.shape[0]):
            Wx = x @ Ws[h] + Wb[h]
            d = Wx.shape[-1]
            s = Wx[v_tgt] @ a_w[h, :d] + Wx[v_src] @ a_w[h, d:] + a_b[h]
            s = jax.nn.leaky_relu(s, negative_slope=0.2)
            alpha = _segment_softmax(s, v_tgt, n)
            outs.append(jax.ops.segment_sum(alpha[:, None] * Wx[v_src], v_tgt, num_segments=n))
        return jnp.stack(outs, axis=1).reshape(n, -1)

    def _L2_gnn_ref(x, edge_index, W_l, b_l, W_r, gamma, beta):
        import jax, jax.numpy as jnp
        import numpy as np
        N_NODES = 50000
        N_EDGES = 25000
        D_IN = 512
        D_OUT = 512
        EPS = 1e-05
        N = x.shape[0]
        src = edge_index[0]
        dst = edge_index[1]
        agg = jax.ops.segment_sum(x[src], dst, num_segments=N)
        deg = jax.ops.segment_sum(jnp.ones_like(dst, jnp.float32), dst, num_segments=N)
        mean_nb = agg / jnp.maximum(deg, 1.0)[:, None]
        h = mean_nb @ W_l.T + b_l + x @ W_r.T
        h = jax.nn.relu(h)
        mu = jnp.mean(h, axis=0)
        var = jnp.mean((h - mu) ** 2, axis=0)
        out = (h - mu) * jax.lax.rsqrt(var + EPS) * gamma + beta
        return out

    def _L3_gnn_ref(x, vals, weight, row, col):
        import jax, jax.numpy as jnp
        import numpy as np
        N_NODES = 625
        N_EDGES = 5000
        N_IN = 512
        N_OUT = 512
        n = x.shape[0]
        msgs = x[col] * vals[:, None]
        agg = jax.ops.segment_sum(msgs, row, num_segments=n)
        return jnp.einsum('nd,od->no', agg, weight)
    edge_index = jnp.stack([src, dst])
    h = jnp.maximum(_layernorm(x, axis=-1), 0.0)
    x = x + _L0_gnn_ref(h, edge_index, L0_gnn_W, L0_gnn_b, L0_gnn_diffusion_weights)
    h = jnp.maximum(_layernorm(x, axis=-1), 0.0)
    x = x + _L1_gnn_ref(h, edge_index, L1_gnn_Ws, L1_gnn_Wb, L1_gnn_a_w, L1_gnn_a_b)
    h = jnp.maximum(_layernorm(x, axis=-1), 0.0)
    x = x + _L2_gnn_ref(h, edge_index, L2_gnn_W_l, L2_gnn_b_l, L2_gnn_W_r, L2_gnn_gamma, L2_gnn_beta)
    h = jnp.maximum(_layernorm(x, axis=-1), 0.0)
    x = x + _L3_gnn_ref(h, edge_weight, L3_gnn_weight, src, dst)
    return x

_drawn_inputs = setup_inputs


def setup_inputs(seed=0):
    import zlib

    import numpy as np

    out = dict(_drawn_inputs(seed))
    spreads = {'L0_gnn_b': (0.0, 0.1),
     'L0_gnn_diffusion_weights': (0.25, 0.6),
     'L2_gnn_b_l': (0.0, 0.1),
     'L2_gnn_gamma': (1.0, 0.2),
     'L2_gnn_beta': (0.0, 0.1)}
    factors = {'L1_gnn_a_b': 8.0}
    for name, (base, spread) in spreads.items():
        noise = np.random.default_rng([zlib.crc32(name.encode()), seed]).standard_normal(out[name].shape)
        drawn = base * np.exp(spread * noise) if base else spread * noise
        out[name] = jnp.asarray(drawn.astype(out[name].dtype))
    for name, factor in factors.items():
        out[name] = (out[name] * factor).astype(out[name].dtype)
    return out
```

```python
from contextlib import ExitStack

import concourse.bass as bass
from concourse import mybir

ALU = mybir.AluOpType
ACT = mybir.ActivationFunctionType
F32 = mybir.dt.float32
BF16 = mybir.dt.bfloat16
I32 = mybir.dt.int32

P = 128
EPS = 1e-5
SLOPE = 0.2
NO_EDGE = -1e30
CAP = 1e30
TINY = 1e-30


def gnn_program(nc: bass.Bass, x, edges, edge_w, w0, ws, ws_T, wl_T, wr_T, w3_T, rows, cols, out):
    N, D = x.shape
    E = edge_w.shape[0] * edge_w.shape[1]
    H, DP = 8, 64
    NT = N // P
    KT = D // P
    ET = E // P
    PAIRS = ET // 2
    CHUNKS = [(0, 3), (3, 8), (8, 13), (13, PAIRS)]
    HP = H // 2
    CB, CA, CGB = 0, KT, KT + 2 * KT

    with ExitStack() as ctx:
        def sb(name, shape, dt=F32):
            return ctx.enter_context(nc.sbuf_tensor(name, shape, dt))

        sems = {}

        def sem(name):
            sems[name] = ctx.enter_context(nc.semaphore(name))
            return sems[name]

        edges_i = sb("edges_i", [P, 2, ET], I32)
        edges_bf = sb("edges_bf", [P, 2, ET], BF16)
        ew = sb("ew", [P, ET])
        ew_rest = sb("ew_rest", [P, 2, ET])
        ew_part = sb("ew_part", [P, 3, ET], BF16)
        ew_lo32 = sb("ew_lo32", [P, ET])
        node_id = sb("node_id", [P, N, 2], BF16)
        src_hot = sb("src_hot", [P, PAIRS, N, 2], BF16)
        dst_hot = sb("dst_hot", [P, PAIRS, N, 2], BF16)
        most = max(b - a for a, b in CHUNKS)
        src_w = [[sb(f"src_w{i}_{j}", [P, most, N, 2], BF16) for j in range(2)] for i in range(3)]

        xs = [sb(f"x{i}", [P, NT, D]) for i in range(2)]
        xs = [xs[i % 2] for i in range(5)]
        hs = [sb(f"h{i}", [P, NT, D]) for i in range(2)]
        hs = [hs[i % 2] for i in range(4)]
        hT = [sb(f"hT{i}", [P, KT, N]) for i in range(2)]
        hT = [hT[i % 2] for i in range(3)]
        aggT = [sb("aggT", [P, KT, N])] * 2
        w0_s, ws_s, wsT_s, wl_s, wr_s, w3_s = (sb(f"w_{n}", [P, KT, D]) for n in ("l0", "l1", "l1T", "l2l", "l2r", "l3"))
        rows_s = sb("rows_s", [P, rows.shape[1]])
        cols_s = sb("cols_s", [P, cols.shape[1]])
        b0_b = rows_s[:, 0:D]
        wb_b = rows_s[:, D:2 * D]
        dw_b = rows_s[:, 2 * D:2 * D + 4]
        ab_b = rows_s[:, 2 * D + 4:2 * D + 4 + H]

        ident = sb("ident", [P, P])
        eye = sb("eye", [P, NT, N])
        eye_w = [sb(f"eye_w{j}", [P, NT, N]) for j in range(3)]
        eps_s = sb("eps_s", [P, 1])
        warm = sb("warm", [P, 1])
        a_blk = sb("a_blk", [P, KT, 2, 2])
        v_s = sb("v_s", [P, KT, 16])
        tu_bias = sb("tu_bias", [P, KT, 2, 2])

        cnt = sb("cnt", [P, NT, N])
        cnt_T = sb("cnt_T", [P, NT, N])
        sym = sb("sym", [P, NT, N])
        adj_T = sb("adj_T", [P, NT, N])
        adj = sb("adj", [P, NT, N])
        poly = [sb(f"poly{j}", [P, NT, N]) for j in range(2)]
        poly.append(poly[0])
        cnt_mean = sb("cnt_mean", [P, NT, N])
        mask = sb("mask", [P, NT, N])
        weighted_T = sb("weighted_T", [P, NT, N])
        rsum = sb("rsum", [P, NT])
        dinv = sb("dinv", [P, NT])
        deg = sb("deg", [P, NT])
        deg1 = sb("deg1", [P, NT])
        rdeg = sb("rdeg", [P, NT])

        bst = sb("bst", [P, 4, NT, 6])
        bmv = sb("bmv", [P, 4, NT, 2])
        sd = sb("sd", [P, 4, NT])
        rs = sb("rs", [P, 4, NT])
        nmr = sb("nmr", [P, 4, NT])

        hwb = sb("hwb", [P, NT, D])
        tu = sb("tu", [P, NT, KT, 2, 2])
        tuT = sb("tuT", [16, N])
        u5 = sb("u5", [P, NT, H])
        zjunk = sb("zjunk", [P, 2, N])
        zmax = sb("zmax", [P, NT, H])
        top = sb("top", [P, NT, H])
        smax = sb("smax", [P, NT, H])
        shift = sb("shift", [P, NT, 2, H])
        shiftT = sb("shiftT", [16, N])
        wx = sb("wx", [P, NT, H, DP + 1])
        low = w0_s[:].rearrange("p (b r) (t n) -> p b r t n", b=2, t=NT)
        vbuf = wsT_s[:].rearrange("p (b r) (t n) -> p b r t n", b=2, t=NT)
        probs = sb("probs", [P, H, NT, N])
        den = sb("den", [P, NT, H])
        rden = sb("rden", [P, NT, H])

        r_s = probs[:, 0:2].rearrange("p h t n -> p (h t) n")
        y_s = probs[:, 2:4].rearrange("p h t n -> p (h t) n")
        bn6 = sb("bn6", [P, KT, 6])
        bn2 = sb("bn2", [P, KT, 2])
        bn_sd = sb("bn_sd", [P, KT])
        bn_rs = sb("bn_rs", [P, KT])
        bn_sc = sb("bn_sc", [P, KT])
        bn_ms = sb("bn_ms", [P, KT])
        bn_bi = sb("bn_bi", [P, KT])

        bank = [ctx.enter_context(nc.psum_tensor(f"bank{i}", [P, 512], F32)) for i in range(8)]

        def halves(b):
            return bank[b][:, :].rearrange("p (a n) -> p a n", a=2)

        for name in ("ld_edges", "ld_ew", "ld_x0", "ld_x1", "ld_w0", "ld_ws", "ld_wsT", "ld_wl", "ld_wr",
                     "ld_w3", "ld_rows", "ld_cols", "node_ids", "ident_ok", "eye_ok", "eye_w_ok", "ablk_ok", "zero_ok",
                     "edges_ok", "ew_ok", "hot_ok", "srcw0_ok", "srcw1_ok", "srcw2_ok",
                     "counts_pe", "cnt_dve", "cnt_act", "cntT_pe", "cntT_ok", "sym_ok", "dinv_ok", "dinvb_pe",
                     "adjT_ok", "adj_ok", "poly0_ok", "prod1_pe", "poly1_ok", "prod2_pe", "poly2_ok",
                     "mask_ok", "rdeg_ok", "rdegb_pe", "cntmean_ok",
                     "h0T_pe", "h0T_act", "h0T_act2", "hw_pe", "hwb_ok", "mix_pe",
                     "v_pe", "v_ok", "tub_ok", "h1T_pe", "h1T_act", "h1T_dve", "tu_pe", "tu_ok", "tuT_pe", "tuT_ok",
                     "ub_pe", "zmax_ok", "shift_ok", "shiftT_pe", "shiftT_ok", "wx_pe", "wx_ok", "wx_one",
                     "u5_ok", "sb_pe", "low_ok", "lin_ok", "exp_ok", "probs_ok", "att_pe", "x2_ok", "half_ok",
                     "h2T_pe", "h2T_act", "h2T_dve", "agg2_pe", "agg2_act", "agg2_dve", "l2_pe", "relu_ok", "bn_ok", "bnsd_ok",
                     "bnaff_ok", "y_ok", "yT_pe", "weighed_pe", "wT_ok",
                     "agg3_pe", "agg3_act", "agg3_dve", "l3_pe", "x_ok", "warm_ok", "stored", "dve_own", "act_own", "pool_own"):
            sem(name)
        for layer in range(4):
            for name in ("mv", "sd", "nmr", "h_act", "h_dve"):
                sem(f"ln{layer}_{name}")
        S = sems

        block = ctx.enter_context(nc.Block())

        @block.sync
        def _(sp):
            sp.dma_start(edges_i[:], edges).then_inc(S["ld_edges"], 16)
            sp.dma_start(ew[:], edge_w).then_inc(S["ld_ew"], 16)
            sp.dma_start(xs[0][:, 0, :], x[0:P, :]).then_inc(S["ld_x0"], 16)
            sp.dma_start(xs[0][:, 1, :], x[P:N, :]).then_inc(S["ld_x1"], 16)
            sp.dma_start(cols_s[:], cols).then_inc(S["ld_cols"], 16)
            sp.dma_start(rows_s[:], rows.broadcast_to([P, rows.shape[1]])).then_inc(S["ld_rows"], 16)
            for dst, src, name in ((w0_s, w0, "ld_w0"), (wsT_s, ws_T, "ld_wsT"), (ws_s, ws, "ld_ws"),
                                   (wr_s, wr_T, "ld_wr"), (wl_s, wl_T, "ld_wl"), (w3_s, w3_T, "ld_w3")):
                sp.dma_start(dst[:], src.rearrange("(k p) n -> p k n", p=P)).then_inc(S[name], 16)
            for t in range(NT):
                sp.wait_ge(S["x_ok"], t + 1)
                sp.dma_start(out[t * P:(t + 1) * P, :], xs[4][:, t, :]).then_inc(S["stored"], 16)
            sp.wait_ge(S["stored"], 16 * NT)

        @block.gpsimd
        def _(pool):
            nc.gpsimd.iota(node_id[:], pattern=[[1, N], [0, 2]], base=0, channel_multiplier=0,
                           allow_small_or_imprecise_dtypes=True).then_inc(S["node_ids"], 1)
            nc.gpsimd.memset(ident[:], 0.0).then_inc(S["pool_own"], 1)
            nc.gpsimd.memset(eye[:], 0.0).then_inc(S["pool_own"], 1)
            nc.gpsimd.memset(eps_s[:], EPS).then_inc(S["zero_ok"], 1)
            nc.gpsimd.memset(a_blk[:], 0.0).then_inc(S["pool_own"], 1)
            pool.wait_ge(S["pool_own"], 1)
            nc.gpsimd.affine_select(out=ident[:], in_=ident[:], compare_op=ALU.not_equal, fill=1.0, base=0,
                                    pattern=[[-1, P]], channel_multiplier=1).then_inc(S["ident_ok"], 1)
            pool.wait_ge(S["pool_own"], 3)
            nc.gpsimd.affine_select(out=eye[:], in_=eye[:], compare_op=ALU.not_equal, fill=1.0, base=0,
                                    pattern=[[P, NT], [-1, N]], channel_multiplier=1).then_inc(S["eye_ok"], 1)
            nc.gpsimd.memset(wx[:, :, :, DP:DP + 1], 1.0).then_inc(S["wx_one"], 1)
            pool.wait_ge(S["ld_cols"], 16)
            pool.wait_ge(S["eye_ok"], 1)
            pool.wait_ge(S["wx_one"], 1)
            for half in range(2):
                part = slice(half * DP, (half + 1) * DP)
                nc.gpsimd.tensor_copy(a_blk[part, :, :, half], cols_s[part, CA:CGB].rearrange("p (k j) -> p k j", j=2)
                                      ).then_inc(S["ablk_ok"], 1)
            pool.wait_ge(S["ld_rows"], 16)
            pool.wait_ge(S["ablk_ok"], 2)
            for n, j in enumerate((2, 1, 0)):
                if n:
                    pool.wait_ge(S["eye_w_ok"], n)
                nc.gpsimd.tensor_scalar(eye_w[j][:], eye[:], dw_b[:, j:j + 1], None, ALU.mult).then_inc(S["eye_w_ok"], 1)
            pool.wait_ge(S["ew_ok"], 3)
            pool.wait_ge(S["eye_w_ok"], 3)
            for c, (a, b) in enumerate(CHUNKS):
                pool.wait_ge(S["hot_ok"], 2 * c + 2)
                if c:
                    pool.wait_ge(S["srcw1_ok"], c)
                if c >= 2:
                    pool.wait_ge(S["weighed_pe"], c - 1)
                nc.gpsimd.tensor_tensor(
                    src_w[1][c % 2][:, 0:b - a], src_hot[:, a:b],
                    ew_part[:, 1, 2 * a:2 * b].rearrange("p (g i) -> p g i", i=2).unsqueeze(2).broadcast_to([P, b - a, N, 2]),
                    ALU.mult).then_inc(S["srcw1_ok"], 1)

        @block.scalar
        def _(act):
            def layernorm_act(layer):
                act.wait_ge(S[f"ln{layer}_mv"], NT)
                nc.scalar.activation(sd[:, layer, :], bmv[:, layer, :, 1], ACT.Sqrt, bias=eps_s[:, 0:1]).then_inc(S[f"ln{layer}_sd"], 1)
                act.wait_ge(S[f"ln{layer}_nmr"], 1)
                nc.scalar.activation(hs[layer][:, 0, :], xs[layer][:, 0, :], ACT.Relu, bias=nmr[:, layer, 0:1],
                                     scale=rs[:, layer, 0:1]).then_inc(S[f"ln{layer}_h_act"], 1)

            def weight_low(c):
                a, b = CHUNKS[c]
                if c >= 2:
                    act.wait_ge(S["weighed_pe"], c - 1)
                for g in range(a, b):
                    for i in range(2):
                        last = nc.scalar.activation(src_w[2][c % 2][:, g - a, :, i], src_hot[:, g, :, i], ACT.Copy,
                                                    scale=ew_lo32[:, 2 * g + i:2 * g + i + 1])
                last.then_inc(S["srcw2_ok"], 1)

            act.wait_ge(S["zero_ok"], 1)
            layernorm_act(0)
            for j in range(2):
                act.wait_ge(S["h0T_pe"], j + 1)
                nc.scalar.copy(hT[0][:, 2 * j:2 * j + 2, :], halves(4 + j)).then_inc(S["h0T_act"], 1)
            act.wait_ge(S["counts_pe"], 2)
            nc.scalar.copy(cnt[:, 1, :], bank[1][:, 0:N]).then_inc(S["cnt_act"], 1)
            act.wait_ge(S["v_pe"], 1)
            nc.scalar.copy(v_s[:], bank[2][:, 0:64].rearrange("p (k c) -> p k c", k=KT)).then_inc(S["v_ok"], 1)
            act.wait_ge(S["dinv_ok"], 1)
            act.wait_ge(S["sym_ok"], NT)
            for t in range(NT):
                nc.scalar.activation(adj[:, t, :], sym[:, t, :], ACT.Copy, scale=dinv[:, t:t + 1]).then_inc(S["adj_ok"], 1)
            act.wait_ge(S["ew_ok"], 3)
            for c in range(3):
                weight_low(c)
            layernorm_act(1)
            act.wait_ge(S["h1T_pe"], 2)
            nc.scalar.copy(hT[1][:, 0:2, :], halves(4)).then_inc(S["h1T_act"], 1)
            act.wait_ge(S["tuT_pe"], 1)
            nc.scalar.copy(tuT[:], bank[3][0:16, 0:N]).then_inc(S["tuT_ok"], 1)
            nc.scalar.activation(warm[:], eps_s[:], ACT.Exp).then_inc(S["warm_ok"], 1)
            weight_low(3)
            act.wait_ge(S["shiftT_pe"], 1)
            nc.scalar.copy(shiftT[:], bank[3][0:16, 0:N]).then_inc(S["shiftT_ok"], 1)
            act.wait_ge(S["u5_ok"], 1)
            for g in range(HP):
                for r in range(2):
                    for st in range(NT):
                        act.wait_ge(S["sb_pe"], g + 1)
                        if g >= 2:
                            act.wait_ge(S["lin_ok"], g - 1)
                        h = 2 * g + r
                        last = nc.scalar.activation(low[:, g % 2, r, st, :], halves(6 + g % 2)[:, r, :], ACT.Identity,
                                                    bias=u5[:, st, h:h + 1])
                last.then_inc(S["low_ok"], 1)
                act.wait_ge(S["lin_ok"], g + 1)
                if g >= 2:
                    act.wait_ge(S["probs_ok"], g - 1)
                nc.scalar.activation(vbuf[:, g % 2], vbuf[:, g % 2], ACT.Exp).then_inc(S["exp_ok"], 1)
            nc.scalar.activation(warm[:], eps_s[:], ACT.Sqrt).then_inc(S["warm_ok"], 1)
            layernorm_act(2)
            act.wait_ge(S["h2T_pe"], 2)
            nc.scalar.copy(hT[2][:, 0:2, :], halves(4)).then_inc(S["h2T_act"], 1)
            act.wait_ge(S["agg2_pe"], 2)
            nc.scalar.copy(aggT[0][:, 0:2, :], halves(2)).then_inc(S["agg2_act"], 1)
            for m in range(KT):
                act.wait_ge(S["l2_pe"], m + 1)
                nc.scalar.activation(r_s[:, m, :], bank[4 + m][:, 0:N], ACT.Relu,
                                     bias=cols_s[:, CGB + m:CGB + m + 1]).then_inc(S["relu_ok"], 1)
                act.wait_ge(S["bn_ok"], m + 1)
                nc.scalar.activation(bn_sd[:, m:m + 1], bn2[:, m, 1:2], ACT.Sqrt, bias=eps_s[:, 0:1]).then_inc(S["bnsd_ok"], 1)
            layernorm_act(3)
            act.wait_ge(S["agg3_pe"], 2)
            nc.scalar.copy(aggT[1][:, 0:2, :], halves(4)).then_inc(S["agg3_act"], 1)

        @block.vector
        def _(dve):
            own = [0]

            def then(ins):
                own[0] += 1
                ins.then_inc(S["dve_own"], 1)
                dve.wait_ge(S["dve_own"], own[0])

            def layernorm_stats(layer, ready):
                for t in range(NT):
                    ready(t)
                    then(nc.vector.bn_stats(bst[:, layer, t, :], xs[layer][:, t, :]))
                    nc.vector.bn_aggr(bmv[:, layer, t, :], bst[:, layer, t, :]).then_inc(S[f"ln{layer}_mv"], 1)

            def layernorm_apply(layer):
                dve.wait_ge(S[f"ln{layer}_sd"], 1)
                then(nc.vector.reciprocal(rs[:, layer, :], sd[:, layer, :]))
                nc.vector.scalar_tensor_tensor(out=nmr[:, layer, :], in0=bmv[:, layer, :, 0], scalar=-1.0, in1=rs[:, layer, :],
                                               op0=ALU.mult, op1=ALU.mult).then_inc(S[f"ln{layer}_nmr"], 1)
                dve.wait_ge(S[f"ln{layer}_nmr"], 1)
                then(nc.vector.tensor_scalar(hs[layer][:, 1, :], xs[layer][:, 1, :], rs[:, layer, 1:2], nmr[:, layer, 1:2],
                                             ALU.mult, ALU.add))
                nc.vector.tensor_scalar(hs[layer][:, 1, :], hs[layer][:, 1, :], 0.0, None, ALU.max).then_inc(S[f"ln{layer}_h_dve"], 1)

            def one_hot(hot, which, c):
                a, b = CHUNKS[c]
                idx = edges_bf[:, which, 2 * a:2 * b].rearrange("p (g i) -> p g i", i=2)
                nc.vector.tensor_tensor(hot[:, a:b], idx.unsqueeze(2).broadcast_to([P, b - a, N, 2]),
                                        node_id[:].unsqueeze(1).broadcast_to([P, b - a, N, 2]), ALU.is_equal).then_inc(S["hot_ok"], 1)

            def weight_high(c):
                a, b = CHUNKS[c]
                part = ew_part[:, 0, 2 * a:2 * b].rearrange("p (g i) -> p g i", i=2)
                if c >= 2:
                    dve.wait_ge(S["weighed_pe"], c - 1)
                nc.vector.tensor_tensor(src_w[0][c % 2][:, 0:b - a], src_hot[:, a:b], part.unsqueeze(2).broadcast_to([P, b - a, N, 2]),
                                        ALU.mult).then_inc(S["srcw0_ok"], 1)

            dve.wait_ge(S["ld_edges"], 16)
            then(nc.vector.tensor_copy(edges_bf[:], edges_i[:]))
            dve.wait_ge(S["node_ids"], 1)
            one_hot(dst_hot, 1, 0)
            one_hot(src_hot, 0, 0)

            layernorm_stats(0, lambda t: dve.wait_ge(S[f"ld_x{t}"], 16))
            one_hot(dst_hot, 1, 1)
            one_hot(src_hot, 0, 1)
            layernorm_apply(0)
            one_hot(dst_hot, 1, 2)
            one_hot(src_hot, 0, 2)
            dve.wait_ge(S["ld_ew"], 16)
            nc.vector.tensor_copy(ew_part[:, 0, :], ew[:]).then_inc(S["ew_ok"], 1)
            dve.wait_ge(S["ew_ok"], 1)
            then(nc.vector.tensor_tensor(ew_rest[:, 0, :], ew[:], ew_part[:, 0, :], ALU.subtract))
            nc.vector.tensor_copy(ew_part[:, 1, :], ew_rest[:, 0, :]).then_inc(S["ew_ok"], 1)
            dve.wait_ge(S["ew_ok"], 2)
            nc.vector.tensor_tensor(ew_lo32[:], ew_rest[:, 0, :], ew_part[:, 1, :], ALU.subtract).then_inc(S["ew_ok"], 1)
            one_hot(dst_hot, 1, 3)
            one_hot(src_hot, 0, 3)

            dve.wait_ge(S["counts_pe"], 1)
            nc.vector.tensor_copy(cnt[:, 0, :], bank[0][:, 0:N]).then_inc(S["cnt_dve"], 1)
            weight_high(0)
            dve.wait_ge(S["cntT_pe"], 1)
            dve.wait_ge(S["cnt_dve"], 1)
            dve.wait_ge(S["cnt_act"], 1)
            for t in range(NT):
                nc.vector.tensor_scalar(cnt_T[:, t, :], halves(3)[:, t, :], 1.0, 0.0, ALU.mult, ALU.add,
                                        accum_out=deg[:, t:t + 1]).then_inc(S["cntT_ok"], 1)
            dve.wait_ge(S["cntT_ok"], NT)
            then(nc.vector.tensor_tensor(sym[:], cnt[:], cnt_T[:], ALU.add))
            dve.wait_ge(S["eye_ok"], 1)
            for t in range(NT):
                nc.vector.scalar_tensor_tensor(out=sym[:, t, :], in0=sym[:, t, :], scalar=1.0, in1=eye[:, t, :], op0=ALU.min,
                                               op1=ALU.add, accum_out=rsum[:, t:t + 1]).then_inc(S["sym_ok"], 1)
            dve.wait_ge(S["sym_ok"], NT)
            then(nc.vector.tensor_scalar(rsum[:], rsum[:], 1.0, None, ALU.max))
            nc.vector.reciprocal(dinv[:], rsum[:]).then_inc(S["dinv_ok"], 1)
            then(nc.vector.tensor_scalar(deg1[:], deg[:], 1.0, None, ALU.max))
            nc.vector.reciprocal(rdeg[:], deg1[:]).then_inc(S["rdeg_ok"], 1)
            dve.wait_ge(S["dinvb_pe"], 1)
            nc.vector.tensor_tensor(adj_T[:], sym[:], bank[0][:, 0:N].unsqueeze(1).broadcast_to([P, NT, N]), ALU.mult
                                    ).then_inc(S["adjT_ok"], 1)
            dve.wait_ge(S["adjT_ok"], 1)
            dve.wait_ge(S["eye_w_ok"], 3)
            nc.vector.scalar_tensor_tensor(out=poly[0][:], in0=adj_T[:], scalar=dw_b[:, 3:4], in1=eye_w[2][:], op0=ALU.mult,
                                           op1=ALU.add).then_inc(S["poly0_ok"], 1)
            dve.wait_ge(S["v_pe"], 1)
            dve.wait_ge(S["v_ok"], 1)
            ab_v = ab_b.rearrange("p (k f) -> p k f", f=2)
            tub = bank[2][:, 64:80].rearrange("p (k j f) -> p k j f", k=KT, j=2)
            nc.vector.tensor_tensor(tu_bias[:, :, 0, :], tub[:, :, 0, :], ab_v, ALU.add).then_inc(S["tub_ok"], 1)
            nc.vector.tensor_copy(tu_bias[:, :, 1, :], tub[:, :, 1, :]).then_inc(S["tub_ok"], 1)
            dve.wait_ge(S["hw_pe"], 1)
            nc.vector.tensor_tensor(hwb[:, 0, :], bank[6][:], b0_b, ALU.add).then_inc(S["hwb_ok"], 1)
            dve.wait_ge(S["prod1_pe"], 1)
            nc.vector.tensor_tensor(poly[1][:], halves(4), eye_w[1][:], ALU.add).then_inc(S["poly1_ok"], 1)
            dve.wait_ge(S["hw_pe"], 2)
            nc.vector.tensor_tensor(hwb[:, 1, :], bank[7][:], b0_b, ALU.add).then_inc(S["hwb_ok"], 1)
            dve.wait_ge(S["prod2_pe"], 1)
            nc.vector.tensor_tensor(poly[2][:], halves(5), eye_w[0][:], ALU.add).then_inc(S["poly2_ok"], 1)
            nc.vector.tensor_scalar(mask[:], cnt_T[:], 0.0, NO_EDGE, ALU.is_equal, ALU.mult).then_inc(S["mask_ok"], 1)
            dve.wait_ge(S["rdegb_pe"], 1)
            nc.vector.tensor_tensor(cnt_mean[:], cnt[:], bank[1][:, 0:N].unsqueeze(1).broadcast_to([P, NT, N]), ALU.mult
                                    ).then_inc(S["cntmean_ok"], 1)
            weight_high(1)
            weight_high(2)

            def residual_0(t):
                dve.wait_ge(S["mix_pe"], t + 1)
                then(nc.vector.scalar_tensor_tensor(out=xs[1][:, t, :], in0=bank[6 + t][:], scalar=0.0, in1=xs[0][:, t, :],
                                                    op0=ALU.max, op1=ALU.add))

            layernorm_stats(1, residual_0)
            layernorm_apply(1)
            dve.wait_ge(S["h1T_pe"], 2)
            nc.vector.tensor_copy(hT[1][:, 2:4, :], halves(5)).then_inc(S["h1T_dve"], 1)
            dve.wait_ge(S["tu_pe"], 1)
            dve.wait_ge(S["tub_ok"], 2)
            nc.vector.tensor_tensor(tu[:].rearrange("p t k j f -> p t (k j f)"), bank[3][:, 0:32].rearrange("p (t c) -> p t c", t=NT),
                                    tu_bias[:].rearrange("p k j f -> p (k j f)").unsqueeze(1).broadcast_to([P, NT, 16]),
                                    ALU.add).then_inc(S["tu_ok"], 1)
            dve.wait_ge(S["tu_ok"], 1)
            nc.vector.tensor_scalar(u5[:].rearrange("p t (k f) -> p t k f", f=2), tu[:, :, :, 1, :], SLOPE, None, ALU.mult
                                    ).then_inc(S["u5_ok"], 1)
            dve.wait_ge(S["mask_ok"], 1)
            for g in range(HP):
                dve.wait_ge(S["ub_pe"], g + 1)
                for r in range(2):
                    for dt in range(NT):
                        n = 4 * g + 2 * r + dt
                        if n >= 2:
                            dve.wait_ge(S["zmax_ok"], n - 1)
                        nc.vector.tensor_tensor_reduce(
                            out=zjunk[:, dt, :], in0=halves(4 + g)[:, r, :], in1=mask[:, dt, :], scale=1.0, scalar=2 * NO_EDGE,
                            op0=ALU.add, op1=ALU.max, accum_out=zmax[:, dt, 2 * g + r:2 * g + r + 1]).then_inc(S["zmax_ok"], 1)
            dve.wait_ge(S["zmax_ok"], 2 * H)
            t_v = tu[:, :, :, 0, :]

            def heads(ap):
                return ap.rearrange("p t (k f) -> p t k f", f=2)

            then(nc.vector.tensor_tensor(heads(top[:]), t_v, heads(zmax[:]), ALU.add))
            then(nc.vector.scalar_tensor_tensor(out=smax[:], in0=top[:], scalar=SLOPE, in1=top[:], op0=ALU.mult, op1=ALU.max))
            for dt in range(NT):
                nc.vector.tensor_tensor(shift[:, dt, 0, :].rearrange("p (k f) -> p k f", f=2), t_v[:, dt],
                                        smax[:, dt, :].rearrange("p (k f) -> p k f", f=2), ALU.subtract).then_inc(S["shift_ok"], 1)
                nc.vector.scalar_tensor_tensor(out=shift[:, dt, 1, :].rearrange("p (k f) -> p k f", f=2), in0=t_v[:, dt],
                                               scalar=SLOPE, in1=smax[:, dt, :].rearrange("p (k f) -> p k f", f=2),
                                               op0=ALU.mult, op1=ALU.subtract).then_inc(S["shift_ok"], 1)
            for t in range(NT):
                dve.wait_ge(S["wx_pe"], t + 1)
                nc.vector.tensor_tensor(wx[:, t, :, 0:DP], bank[t][:].rearrange("p (h d) -> p h d", d=DP),
                                        wb_b.rearrange("p (h d) -> p h d", d=DP), ALU.add).then_inc(S["wx_ok"], 1)

            weight_high(3)

            def scores(g):
                dve.wait_ge(S["low_ok"], g + 1)
                for r in range(2):
                    for st in range(NT):
                        h = 2 * g + r
                        last = nc.vector.scalar_tensor_tensor(
                            out=vbuf[:, g % 2, r, st, :], in0=halves(4 + g % 2)[:, r, :],
                            scalar=tu[:, st, g, 1, r:r + 1], in1=low[:, g % 2, r, st, :], op0=ALU.add, op1=ALU.max)
                last.then_inc(S["lin_ok"], 1)

            def times_counts(g):
                dve.wait_ge(S["exp_ok"], g + 1)
                nc.vector.scalar_tensor_tensor(
                    out=probs[:, 2 * g:2 * g + 2].rearrange("p h t n -> p h (t n)"),
                    in0=vbuf[:, g % 2].rearrange("p h t n -> p h (t n)"), scalar=CAP,
                    in1=cnt[:].rearrange("p t n -> p (t n)").unsqueeze(1).broadcast_to([P, 2, NT * N]),
                    op0=ALU.min, op1=ALU.mult).then_inc(S["probs_ok"], 1)

            def attention_out(half):
                for dt in range(NT):
                    dve.wait_ge(S["att_pe"], NT * half + dt + 1)
                    o = bank[dt][:, 0:4 * (DP + 1)].rearrange("p (h d) -> p h d", d=DP + 1)
                    hh = slice(4 * half, 4 * half + 4)
                    then(nc.vector.tensor_scalar(den[:, dt, hh], o[:, :, DP], TINY, None, ALU.max))
                    then(nc.vector.reciprocal(rden[:, dt, hh], den[:, dt, hh]))
                    for i in range(4):
                        h = 4 * half + i
                        last = nc.vector.scalar_tensor_tensor(
                            out=xs[2][:, dt, h * DP:(h + 1) * DP], in0=o[:, i, 0:DP], scalar=rden[:, dt, h:h + 1],
                            in1=xs[1][:, dt, h * DP:(h + 1) * DP], op0=ALU.mult, op1=ALU.add)
                    last.then_inc(S["x2_ok"], 1)

            scores(0)
            for g in range(HP):
                if g + 1 < HP:
                    if g + 1 >= 2:
                        dve.wait_ge(S["probs_ok"], g)
                    scores(g + 1)
                times_counts(g)
                if g == 2:
                    attention_out(0)
            dve.wait_ge(S["weighed_pe"], len(CHUNKS))
            nc.vector.tensor_copy(weighted_T[:], halves(2)).then_inc(S["wT_ok"], 1)
            attention_out(1)

            layernorm_stats(2, lambda t: dve.wait_ge(S["x2_ok"], NT + t + 1))
            layernorm_apply(2)
            dve.wait_ge(S["h2T_pe"], 2)
            nc.vector.tensor_copy(hT[2][:, 2:4, :], halves(5)).then_inc(S["h2T_dve"], 1)
            dve.wait_ge(S["agg2_pe"], 2)
            nc.vector.tensor_copy(aggT[0][:, 2:4, :], halves(3)).then_inc(S["agg2_dve"], 1)
            for m in range(KT):
                dve.wait_ge(S["relu_ok"], m + 1)
                then(nc.vector.bn_stats(bn6[:, m, :], r_s[:, m, :]))
                nc.vector.bn_aggr(bn2[:, m, :], bn6[:, m, :]).then_inc(S["bn_ok"], 1)
                dve.wait_ge(S["bnsd_ok"], m + 1)
                one = slice(m, m + 1)
                then(nc.vector.reciprocal(bn_rs[:, one], bn_sd[:, one]))
                then(nc.vector.tensor_tensor(bn_sc[:, one], bn_rs[:, one], cols_s[:, CGB + KT + m:CGB + KT + m + 1], ALU.mult))
                then(nc.vector.tensor_tensor(bn_ms[:, one], bn2[:, m, 0:1], bn_sc[:, one], ALU.mult))
                then(nc.vector.tensor_tensor(bn_bi[:, one], cols_s[:, CGB + 2 * KT + m:CGB + 2 * KT + m + 1], bn_ms[:, one], ALU.subtract))
                nc.vector.tensor_scalar(y_s[:, m, :], r_s[:, m, :], bn_sc[:, one], bn_bi[:, one], ALU.mult, ALU.add
                                        ).then_inc(S["y_ok"], 1)

            def residual_2(t):
                dve.wait_ge(S["yT_pe"], t + 1)
                then(nc.vector.tensor_tensor(xs[3][:, t, :], bank[t][:], xs[2][:, t, :], ALU.add))

            layernorm_stats(3, residual_2)
            layernorm_apply(3)
            dve.wait_ge(S["agg3_pe"], 2)
            nc.vector.tensor_copy(aggT[1][:, 2:4, :], halves(5)).then_inc(S["agg3_dve"], 1)
            for t in range(NT):
                dve.wait_ge(S["l3_pe"], t + 1)
                nc.vector.tensor_tensor(xs[4][:, t, :], bank[6 + t][:], xs[3][:, t, :], ALU.add).then_inc(S["x_ok"], 1)

        @block.tensor
        def _(pe):
            def count_edges(c):
                pe.wait_ge(S["hot_ok"], 2 * c + 2)
                for g in range(*CHUNKS[c]):
                    for i in range(2):
                        for half in range(NT):
                            last = nc.tensor.matmul(bank[half][:, 0:N], src_hot[:, g, half * P:(half + 1) * P, i],
                                                    dst_hot[:, g, :, i], start=(g + i == 0), stop=(g == PAIRS - 1 and i == 1))
                            if g == PAIRS - 1 and i == 1:
                                last.then_inc(S["counts_pe"], 1)

            def weigh_edges(c):
                if c == 0:
                    pe.wait_ge(S["tub_ok"], 2)
                for part in range(3):
                    pe.wait_ge(S[f"srcw{part}_ok"], c + 1)
                a, b = CHUNKS[c]
                for g in range(a, b):
                    for i in range(2):
                        for half in range(NT):
                            for part in range(3):
                                last = nc.tensor.matmul(halves(2)[:, half, :], dst_hot[:, g, half * P:(half + 1) * P, i],
                                                        src_w[part][c % 2][:, g - a, :, i], start=(g + i + half + part == 0),
                                                        stop=(g == PAIRS - 1 and i == 1 and part == 2), skip_group_check=True)
                last.then_inc(S["weighed_pe"], 1)

            def transpose_h(layer, name):
                for t in range(NT):
                    pe.wait_ge(S[f"ln{layer}_" + ("h_act", "h_dve")[t]], 1)
                    for k in range(KT):
                        last = nc.tensor.transpose(halves(4 + k // 2)[:, k % 2, t * P:(t + 1) * P],
                                                   hs[layer][:, t, k * P:(k + 1) * P], ident[:])
                        if t == NT - 1 and k % 2:
                            last.then_inc(S[name], 1)

            def project_0(t):
                for k in range(KT):
                    last = nc.tensor.matmul(bank[6 + t][:], hT[0][:, k, t * P:(t + 1) * P], w0_s[:, k, :], start=(k == 0), stop=(k == KT - 1))
                last.then_inc(S["hw_pe"], 1)

            def row_of(bank_ap, col_of):
                for t in range(NT):
                    last = nc.tensor.matmul(bank_ap[:, t * P:(t + 1) * P], col_of(t).broadcast_to([P, P]), ident[:], start=True, stop=True)
                return last

            def adj_T_times(mat, out_halves):
                for m in range(NT):
                    for k in range(NT):
                        last = nc.tensor.matmul(out_halves[:, m, :], adj[:, k, m * P:(m + 1) * P], mat[:, k, :], start=(k == 0), stop=(k == NT - 1))
                return last

            def aggregate_T(layer, mat, banks, name):
                for k in range(KT):
                    for t in range(NT):
                        last = nc.tensor.matmul(halves(banks[k // 2])[:, k % 2, :], hs[layer][:, t, k * P:(k + 1) * P], mat[:, t, :],
                                                start=(t == 0), stop=(t == NT - 1))
                    if k % 2:
                        last.then_inc(S[name], 1)

            count_edges(0)
            pe.wait_ge(S["ident_ok"], 1)
            count_edges(1)
            transpose_h(0, "h0T_pe")
            count_edges(2)
            count_edges(3)

            pe.wait_ge(S["ld_wsT"], 16)
            pe.wait_ge(S["ablk_ok"], 2)
            for m in range(KT):
                for k in range(KT):
                    nc.tensor.matmul(bank[2][:, 16 * m + 4 * k:16 * m + 4 * k + 4], wsT_s[:, k, m * P:(m + 1) * P],
                                     a_blk[:, k].rearrange("p j f -> p (j f)"), start=True, stop=True)
            for k in range(KT):
                last = nc.tensor.matmul(bank[2][:, 64 + 4 * k:64 + 4 * k + 4], cols_s[:, CB + k:CB + k + 1].broadcast_to([P, P]),
                                        a_blk[:, k].rearrange("p j f -> p (j f)"), start=True, stop=True)
            last.then_inc(S["v_pe"], 1)

            pe.wait_ge(S["cnt_dve"], 1)
            pe.wait_ge(S["cnt_act"], 1)
            for a in range(NT):
                for b in range(NT):
                    last = nc.tensor.transpose(halves(3)[:, b, a * P:(a + 1) * P], cnt[:, a, b * P:(b + 1) * P], ident[:])
            last.then_inc(S["cntT_pe"], 1)

            pe.wait_ge(S["ld_w0"], 16)
            pe.wait_ge(S["h0T_act"], 2)
            project_0(0)
            pe.wait_ge(S["dinv_ok"], 1)
            row_of(bank[0], lambda t: dinv[:, t:t + 1]).then_inc(S["dinvb_pe"], 1)
            pe.wait_ge(S["rdeg_ok"], 1)
            row_of(bank[1], lambda t: rdeg[:, t:t + 1]).then_inc(S["rdegb_pe"], 1)
            project_0(1)
            pe.wait_ge(S["adj_ok"], NT)
            pe.wait_ge(S["poly0_ok"], 1)
            adj_T_times(poly[0], halves(4)).then_inc(S["prod1_pe"], 1)
            weigh_edges(0)
            pe.wait_ge(S["poly1_ok"], 1)
            adj_T_times(poly[1], halves(5)).then_inc(S["prod2_pe"], 1)
            pe.wait_ge(S["poly2_ok"], 1)
            pe.wait_ge(S["hwb_ok"], 2)
            for t in range(NT):
                for k in range(NT):
                    last = nc.tensor.matmul(bank[6 + t][:], poly[2][:, k, t * P:(t + 1) * P], hwb[:, k, :], start=(k == 0), stop=(k == NT - 1))
                last.then_inc(S["mix_pe"], 1)

            weigh_edges(1)

            transpose_h(1, "h1T_pe")
            pe.wait_ge(S["h1T_act"], 1)
            pe.wait_ge(S["h1T_dve"], 1)
            pe.wait_ge(S["v_ok"], 1)
            for t in range(NT):
                for k in range(KT):
                    last = nc.tensor.matmul(bank[3][:, 16 * t:16 * t + 16], hT[1][:, k, t * P:(t + 1) * P], v_s[:, k, :], start=(k == 0), stop=(k == KT - 1))
            last.then_inc(S["tu_pe"], 1)
            pe.wait_ge(S["ld_ws"], 16)
            pe.wait_ge(S["cntmean_ok"], 1)
            for t in range(NT):
                for k in range(KT):
                    last = nc.tensor.matmul(bank[t][:], hT[1][:, k, t * P:(t + 1) * P], ws_s[:, k, :], start=(k == 0), stop=(k == KT - 1))
                last.then_inc(S["wx_pe"], 1)
                if t == 0:
                    pe.wait_ge(S["tu_ok"], 1)
                    for tt in range(NT):
                        tr = nc.tensor.transpose(bank[3][0:16, tt * P:(tt + 1) * P], tu[:, tt].rearrange("p k j f -> p (k j f)"), ident[:])
                    tr.then_inc(S["tuT_pe"], 1)
                    pe.wait_ge(S["tuT_ok"], 1)
                    for g in range(HP):
                        for r in range(2):
                            row = 4 * g + 2 + r
                            last = nc.tensor.matmul(halves(4 + g)[:, r, :], ident[0:16, row:row + 1].broadcast_to([16, P]), tuT[:], start=True, stop=True)
                        last.then_inc(S["ub_pe"], 1)

            pe.wait_ge(S["shift_ok"], 2 * NT)
            for tt in range(NT):
                tr = nc.tensor.transpose(bank[3][0:16, tt * P:(tt + 1) * P], shift[:, tt].rearrange("p j h -> p (j h)"), ident[:])
            tr.then_inc(S["shiftT_pe"], 1)
            pe.wait_ge(S["shiftT_ok"], 1)

            def shift_rows(g):
                for r in range(2):
                    h = 2 * g + r
                    nc.tensor.matmul(halves(4 + g % 2)[:, r, :], ident[0:16, h:h + 1].broadcast_to([16, P]), shiftT[:], start=True, stop=True)
                    last = nc.tensor.matmul(halves(6 + g % 2)[:, r, :], ident[0:16, H + h:H + h + 1].broadcast_to([16, P]), shiftT[:], start=True, stop=True)
                last.then_inc(S["sb_pe"], 1)

            def attend(g):
                pe.wait_ge(S["probs_ok"], g + 1)
                if g == 2:
                    pe.wait_ge(S["x2_ok"], NT)
                for dt in range(NT):
                    for r in range(2):
                        h = 2 * g + r
                        i = h % 4
                        for st in range(NT):
                            last = nc.tensor.matmul(bank[dt][:, i * (DP + 1):(i + 1) * (DP + 1)], probs[:, h, st, dt * P:(dt + 1) * P],
                                                    wx[:, st, h, :], start=(st == 0), stop=(st == NT - 1))
                    if g % 2:
                        last.then_inc(S["att_pe"], 1)

            shift_rows(0)
            shift_rows(1)
            pe.wait_ge(S["wx_ok"], NT)
            pe.wait_ge(S["wx_one"], 1)
            for g in range(HP):
                if g + 2 < HP:
                    pe.wait_ge(S["lin_ok"], g + 1)
                    shift_rows(g + 2)
                if g == 1:
                    weigh_edges(2)
                if g == 3:
                    weigh_edges(3)
                attend(g)

            transpose_h(2, "h2T_pe")
            pe.wait_ge(S["wT_ok"], 1)
            aggregate_T(2, cnt_mean, (2, 3), "agg2_pe")
            pe.wait_ge(S["h2T_act"], 1)
            pe.wait_ge(S["h2T_dve"], 1)
            pe.wait_ge(S["agg2_act"], 1)
            pe.wait_ge(S["agg2_dve"], 1)
            pe.wait_ge(S["ld_wr"], 16)
            pe.wait_ge(S["ld_wl"], 16)
            for m in range(KT):
                for n, (w, right) in enumerate(((wr_s, hT[2]), (wl_s, aggT[0]))):
                    for k in range(KT):
                        last = nc.tensor.matmul(bank[4 + m][:, 0:N], w[:, k, m * P:(m + 1) * P], right[:, k, :],
                                                start=(n == 0 and k == 0), stop=(n == 1 and k == KT - 1))
                last.then_inc(S["l2_pe"], 1)
            for m in range(KT):
                pe.wait_ge(S["y_ok"], m + 1)
                for t in range(NT):
                    last = nc.tensor.transpose(bank[t][:, m * P:(m + 1) * P], y_s[:, m, t * P:(t + 1) * P], ident[:])
                    if m == KT - 1:
                        last.then_inc(S["yT_pe"], 1)

            pe.wait_ge(S["ln3_h_act"], 1)
            pe.wait_ge(S["ln3_h_dve"], 1)
            aggregate_T(3, weighted_T, (4, 5), "agg3_pe")
            pe.wait_ge(S["agg3_act"], 1)
            pe.wait_ge(S["agg3_dve"], 1)
            pe.wait_ge(S["ld_w3"], 16)
            for t in range(NT):
                for k in range(KT):
                    last = nc.tensor.matmul(bank[6 + t][:], aggT[1][:, k, t * P:(t + 1) * P], w3_s[:, k, :], start=(k == 0), stop=(k == KT - 1))
                last.then_inc(S["l3_pe"], 1)


def kernel(x, src, dst, edge_weight, L0_gnn_W, L0_gnn_b, L0_gnn_diffusion_weights, L1_gnn_Ws, L1_gnn_Wb, L1_gnn_a_w,
           L1_gnn_a_b, L2_gnn_W_l, L2_gnn_b_l, L2_gnn_W_r, L2_gnn_gamma, L2_gnn_beta, L3_gnn_weight):
    import numpy as np
    import concourse.bacc as bacc
    from concourse.bass_utils import run_bass_kernel_spmd

    def a(v):
        return np.asarray(v)

    p, d = 128, x.shape[1]
    ws = a(L1_gnn_Ws)
    heads = ws.shape[0]
    dp = ws.shape[2]
    cols = np.concatenate([
        a(L1_gnn_Wb).reshape(heads // 2, 2 * dp).T,
        a(L1_gnn_a_w).reshape(heads // 2, 2, 2, dp).transpose(1, 3, 0, 2).reshape(2 * dp, heads),
        a(L2_gnn_b_l).reshape(d // p, p).T, a(L2_gnn_gamma).reshape(d // p, p).T, a(L2_gnn_beta).reshape(d // p, p).T,
    ], axis=1)
    rows = np.concatenate([a(L0_gnn_b), a(L1_gnn_Wb).reshape(-1), a(L0_gnn_diffusion_weights), a(L1_gnn_a_b)])[None, :]
    arrays = {
        "x": a(x),
        "edges": np.stack([a(src).reshape(p, -1), a(dst).reshape(p, -1)], axis=1),
        "edge_w": a(edge_weight).reshape(p, -1),
        "w0": a(L0_gnn_W),
        "ws": ws.transpose(1, 0, 2).reshape(d, heads * dp),
        "ws_T": ws.transpose(0, 2, 1).reshape(heads * dp, d),
        "wl_T": a(L2_gnn_W_l).T, "wr_T": a(L2_gnn_W_r).T, "w3_T": a(L3_gnn_weight).T,
        "rows": rows, "cols": cols,
    }
    arrays = {f"in_{k}": np.ascontiguousarray(v) for k, v in arrays.items()}
    nc = bacc.Bacc("TRN2", target_bir_lowering=False, num_devices=1)
    ins = [nc.dram_tensor(k, v.shape, mybir.dt.from_np(v.dtype), kind="ExternalInput").ap() for k, v in arrays.items()]
    out = nc.dram_tensor("out", x.shape, F32, kind="ExternalOutput").ap()
    gnn_program(nc, *ins, out)
    done = run_bass_kernel_spmd(nc, [arrays], core_ids=[0])
    return done.results[0]["out"]
```

```python
from contextlib import ExitStack

import concourse.bass as bass
from concourse import mybir

ALU = mybir.AluOpType
ACT = mybir.ActivationFunctionType
F32 = mybir.dt.float32
BF16 = mybir.dt.bfloat16
F32R = mybir.dt.float32r
I32 = mybir.dt.int32

P = 128
EPS = 1e-5
SLOPE = 0.2
STEEP = 4.0
NO_EDGE = -1e30
FLOOR = -1e29
TINY = 1e-30


def gnn_program(nc: bass.Bass, x, edges, edge_w, w0, ws, wl_T, wr_T, w3_T, rows, cols, out):
    N, D = x.shape
    E = edge_w.shape[0] * edge_w.shape[1]
    H, DP = 8, 64
    NT = N // P
    KT = D // P
    ET = E // P
    PAIRS = ET // 2
    CHUNKS = [(0, 1), (1, 5), (5, 9), (9, 12), (12, PAIRS)]
    HP = H // 2
    HALF = H // 2
    ZB = 4
    PIECES = [(0, 0, D, 6), (1, 0, D // 2, 7), (1, D // 2, D, 0)]
    CGB = 0

    with ExitStack() as ctx:
        def sb(name, shape, dt=F32, stack=ctx):
            return stack.enter_context(nc.sbuf_tensor(name, shape, dt))

        sems = {}

        def sem(name):
            sems[name] = ctx.enter_context(nc.semaphore(name))
            return sems[name]

        with ExitStack() as early:
            w0_s = sb("w_l0", [P, KT, D], stack=early)
            prod_s = sb("prod", [P, KT, D], stack=early)
            hwb = sb("hwb", [P, NT, D], stack=early)
            wx = sb("wx", [P, NT, H, DP], stack=early)
        wl_low, wl_high = (sb(f"wl_{part}", [P, KT, D], F32R) for part in ("low", "high"))
        wl_part = [wl_high, wl_low]
        agg2T_part = [sb(f"agg2T_{part}", [P, KT, N], F32R) for part in ("high", "low")]
        edges_i = sb("edges_i", [P, 2, ET], I32)
        edges_bf = sb("edges_bf", [P, 2, ET], BF16)
        ew = sb("ew", [P, ET])
        ew_rest = sb("ew_rest", [P, 2, ET])
        ew_part = sb("ew_part", [P, 3, ET], BF16)
        ew_lo32 = sb("ew_lo32", [P, ET])
        node_id = sb("node_id", [P, N, 2], BF16)
        src_hot = sb("src_hot", [P, PAIRS, N, 2], BF16)
        dst_hot = sb("dst_hot", [P, PAIRS, N, 2], BF16)
        src_w = [src_hot] + [sb(f"src_w{i}", [P, PAIRS, N, 2], BF16) for i in (1, 2)]

        xs = [sb(f"x{i}", [P, NT, D]) for i in range(2)]
        xs = [xs[i % 2] for i in range(5)]
        hs = [sb(f"h{i}", [P, NT, D]) for i in range(2)]
        hs = [hs[i % 2] for i in range(4)]
        ws_s, wl_s, w3_s = (sb(f"w_{n}", [P, KT, D]) for n in ("l1", "l2l", "l3"))
        wr_s = ws_s
        w_part = [sb(f"w_{part}", [P, KT, D], F32R) for part in ("high", "low")]
        xT_part = [sb(f"xT_{part}", [P, KT, N], F32R) for part in ("high", "low")]
        THREE = ((0, 0), (0, 1), (1, 0))
        rows_s = sb("rows_s", [P, rows.shape[1]])
        cols_s = sb("cols_s", [P, cols.shape[1]])
        b0_b = rows_s[:, 0:D]
        wb_b = rows_s[:, D:2 * D]
        dw_b = rows_s[:, 2 * D:2 * D + 4]
        ab_b = rows_s[:, 2 * D + 4:2 * D + 4 + H]
        beta_b = rows_s[:, 2 * D + 4 + H:3 * D + 4 + H]
        a_b = rows_s[:, 3 * D + 4 + H:5 * D + 4 + H].rearrange("p (j n) -> p j n", j=2)

        ident = sb("ident", [P, P])
        eye = sb("eye", [P, NT, N])
        probs = sb("probs", [P, H, NT, N])
        eye_w = {i: probs[:, i - 1] for i in (1, 2)}
        eps_s = sb("eps_s", [P, 1])
        warm = sb("warm", [P, 1])
        prod = [prod_s[:, :, :], probs[:, 4:8].rearrange("p h t n -> p h (t n)")]
        mask = sb("mask", [P, NT, N])
        prod_b = [hs[1][:, 0, :], mask[:].rearrange("p t n -> p (t n)")]
        v_s = sb("v_s", [P, KT + 1, 2, H])
        v_part = [sb(f"v_{part}", [P, KT + 1, 2 * H], F32R) for part in ("high", "low")]
        zeros = sb("zeros", [P, D], BF16)
        wb_part = [sb(f"wb_{part}", [1, D], F32R) for part in ("high", "low")]
        ones_r = sb("ones_r", [1, N], F32R)
        ident_r = sb("ident_r", [16, 16], F32R)

        cnt = sb("cnt", [P, NT, N])
        cnt_T = sb("cnt_T", [P, NT, N])
        sym = probs[:, 2]
        poly = [probs[:, 3], wx[:].rearrange("p t h d -> p (t h d)")[:, 0:NT * N].rearrange("p (t n) -> p t n", t=NT), probs[:, 3]]
        cnt_mean = eye
        weighted_T = cnt_T
        rsum = sb("rsum", [P, NT])
        dinv = sb("dinv", [P, NT])
        dinv_w3 = sb("dinv_w3", [P, NT])
        rsum_w0 = sb("rsum_w0", [P, NT])
        deg = sb("deg", [P, NT])
        deg1 = sb("deg1", [P, NT])
        rdeg = sb("rdeg", [P, NT])

        sum0 = sb("sum0", [P, NT])
        nmean0 = sb("nmean0", [P, NT])
        sq0 = sb("sq0", [P, NT])
        bst = sb("bst", [P, 4, NT, 6])
        bmv = sb("bmv", [P, 4, NT, 2])
        sd = sb("sd", [P, 4, NT])
        rs = sb("rs", [P, 4, NT])
        nmr = sb("nmr", [P, 4, NT])

        tu = sb("tu", [P, NT, 2, H])
        tuT = [sb(f"tuT_{part}", [16, N], F32R) for part in ("high", "low")]
        zmax = sb("zmax", [P, NT, H])
        top = sb("top", [P, NT, H])
        smax = sb("smax", [P, NT, H])
        shift = sb("shift", [P, NT, H])
        t4 = sb("t4", [P, NT, H])
        nt = sb("nt", [P, H])
        z_s, term = ([buf[:, i].rearrange("p (t n) -> p t n", t=NT) for i in range(ZB)] for buf in (prod[0], w0_s))
        den = sb("den", [P, NT, H])
        rden = sb("rden", [P, NT, H])

        r_s = probs[:, 0:2].rearrange("p h t n -> p (h t) n")
        y_s = probs[:, 2:4].rearrange("p h t n -> p (h t) n")
        bn6 = sb("bn6", [P, KT, 6])
        bn2 = sb("bn2", [P, KT, 2])
        bn_sd = sb("bn_sd", [P, KT])
        bn_rs = sb("bn_rs", [P, KT])
        bn_sc = sb("bn_sc", [P, KT])

        bank = [ctx.enter_context(nc.psum_tensor(f"bank{i}", [P, 512], F32)) for i in range(8)]

        def halves(b):
            return bank[b][:, :].rearrange("p (a n) -> p a n", a=2)

        UB = (4, 5, 1, 0)
        TU = 0
        MIX = 4
        ATT = ((4, 5), (0, 1))
        BY_DVE = (5,)
        TB = (3, 6, 7)

        for name in ("ld_edges", "ld_ew", "ld_x0", "ld_x1", "ld_w0", "ld_ws", "ld_wl", "ld_wr",
                     "ld_w3", "ld_rows", "ld_cols", "node_ids", "ident_ok", "eye_ok", "eye_w_ok", "x2_beta", "identr_ok", "prod_ok", "halved_ok", "zero_ok",
                     "edges_ok", "ew_ok", "hot_ok", "srcw0_ok", "counted", "srcw1_ok", "srcw2_ok",
                     "counts_pe", "cnt_act", "cntT_pe", "cntT_ok", "sym_ok", "dinv_ok", "rsum_ok", "y2s_ok",
                     "poly0_ok", "prod1_pe", "poly1_ok", "prod2_pe", "poly2_ok",
                     "mask_ok", "rdeg_ok", "rdegb_pe", "cntmean_ok",
                     "h0T_pe", "h0T_hi", "h0T_lo", "hw_pe", "hwb_ok", "mix_pe", "mixrelu_ok", "sum0_ok", "nmean0_ok", "sq0_ok", "rs0_ok",
                     "v_ok", "vb_ok", "h1T_pe", "h1T_hi", "h1T_lo", "ws_hi", "ws_lo", "wr_hi", "wr_lo", "w3_hi", "w3_lo", "l2r_pe", "v_hi", "v_lo", "tu_pe", "tu_ok", "tuT_pe", "tuT_ok", "tuT_lo", "ones_ok", "wb_hi", "wb_lo", "w0_hi", "w0_lo", "zeros_ok",
                     "ub_pe", "zmax_ok", "top_ok", "smax_ok", "shift_ok", "wx_pe", "wx_ok",
                     "relu4_ok", "steep_dve", "nt_ok", "shift1_ok", "t4_ok", "leaky_ok", "exp_ok", "term_ok", "termT_pe", "probs_act", "probs_dve", "att_pe", "scaled_ok", "x2_ok",
                     "h2T_pe", "h2T_hi", "h2T_lo", "agg2_pe", "agg2_hi", "agg2_lo", "wl_hi", "wl_lo", "l2_pe", "relu_ok", "bn_ok", "bnsd_ok",
                     "bnaff_ok", "y_ok", "yT_pe", "weighed_pe", "wT_ok",
                     "agg3_pe", "agg3_hi", "agg3_lo", "l3_pe", "x_ok", "warm_ok", "stored", "dve_own", "act_own", "pool_own"):
            sem(name)
        for layer in range(4):
            for name in ("mv", "sd", "nmr", "h_act", "h_dve"):
                sem(f"ln{layer}_{name}")
        S = sems

        block = ctx.enter_context(nc.Block())

        @block.sync
        def _(sp):
            sp.dma_start(edges_i[:], edges).then_inc(S["ld_edges"], 16)
            sp.dma_start(ew[:], edge_w).then_inc(S["ld_ew"], 16)
            sp.dma_start(xs[0][:, 0, :], x[0:P, :]).then_inc(S["ld_x0"], 16)
            sp.dma_start(xs[0][:, 1, :], x[P:N, :]).then_inc(S["ld_x1"], 16)
            sp.dma_start(w0_s[:], w0.rearrange("(k p) n -> p k n", p=P)).then_inc(S["ld_w0"], 16)
            sp.dma_start(rows_s[:], rows.broadcast_to([P, rows.shape[1]])).then_inc(S["ld_rows"], 16)
            sp.dma_start(cols_s[:], cols).then_inc(S["ld_cols"], 16)
            for dst, src, name in ((ws_s, ws, "ld_ws"), (wl_s, wl_T, "ld_wl"), (w3_s, w3_T, "ld_w3"), (wr_s, wr_T, "ld_wr")):
                if name == "ld_wr":
                    sp.wait_ge(S["ws_lo"], 1)
                sp.dma_start(dst[:], src.rearrange("(k p) n -> p k n", p=P)).then_inc(S[name], 16)
            for i, (t, a, b, _) in enumerate(PIECES):
                sp.wait_ge(S["x_ok"], i + 1)
                sp.dma_start(out[t * P:(t + 1) * P, a:b], xs[4][:, t, a:b]).then_inc(S["stored"], 16)
            sp.wait_ge(S["stored"], 16 * len(PIECES))

        @block.gpsimd
        def _(pool):
            nc.gpsimd.memset(eps_s[:], EPS).then_inc(S["zero_ok"], 1)
            nc.gpsimd.iota(node_id[:], pattern=[[1, N], [0, 2]], base=0, channel_multiplier=0,
                           allow_small_or_imprecise_dtypes=True).then_inc(S["node_ids"], 1)
            nc.gpsimd.memset(ident[:], 0.0).then_inc(S["pool_own"], 1)
            nc.gpsimd.memset(eye[:], 0.0).then_inc(S["pool_own"], 1)
            pool.wait_ge(S["pool_own"], 2)
            pool.wait_ge(S["ld_ew"], 16)
            nc.gpsimd.tensor_copy(ew_part[:, 0, :], ew[:]).then_inc(S["ew_ok"], 1)
            pool.wait_ge(S["ew_ok"], 1)
            nc.gpsimd.tensor_tensor(ew_rest[:, 0, :], ew[:], ew_part[:, 0, :], ALU.subtract).then_inc(S["pool_own"], 1)
            pool.wait_ge(S["pool_own"], 3)
            nc.gpsimd.tensor_copy(ew_part[:, 1, :], ew_rest[:, 0, :]).then_inc(S["ew_ok"], 1)
            pool.wait_ge(S["ew_ok"], 2)
            nc.gpsimd.tensor_tensor(ew_lo32[:], ew_rest[:, 0, :], ew_part[:, 1, :], ALU.subtract).then_inc(S["ew_ok"], 1)
            pool.wait_ge(S["ew_ok"], 3)
            nc.gpsimd.affine_select(out=ident[:], in_=ident[:], compare_op=ALU.not_equal, fill=1.0, base=0,
                                    pattern=[[-1, P]], channel_multiplier=1).then_inc(S["ident_ok"], 1)
            pool.wait_ge(S["ident_ok"], 1)
            nc.gpsimd.affine_select(out=eye[:], in_=eye[:], compare_op=ALU.not_equal, fill=1.0, base=0,
                                    pattern=[[P, NT], [-1, N]], channel_multiplier=1).then_inc(S["eye_ok"], 1)
            pool.wait_ge(S["eye_ok"], 1)

            def middle_part(c):
                a, b = CHUNKS[c]
                pool.wait_ge(S["hot_ok"], 2 * c + 2)
                nc.gpsimd.tensor_tensor(
                    src_w[1][:, a:b], src_hot[:, a:b],
                    ew_part[:, 1, 2 * a:2 * b].rearrange("p (g i) -> p g i", i=2).unsqueeze(2).broadcast_to([P, b - a, N, 2]),
                    ALU.mult).then_inc(S["srcw1_ok"], 1)
                pool.wait_ge(S["srcw1_ok"], c + 1)

            def score_products(j):
                nc.gpsimd.tensor_tensor(prod[j], ws_s[:], a_b[:, j].unsqueeze(1).broadcast_to([P, KT, D]), ALU.mult
                                        ).then_inc(S["prod_ok"], 1)
                pool.wait_ge(S["prod_ok"], 2 * j + 1)
                nc.gpsimd.tensor_tensor(prod_b[j], wb_b, a_b[:, j], ALU.mult).then_inc(S["prod_ok"], 1)
                pool.wait_ge(S["prod_ok"], 2 * j + 2)

            for c in range(3):
                middle_part(c)
            pool.wait_ge(S["ld_rows"], 16)
            pool.wait_ge(S["ld_ws"], 16)
            score_products(0)
            score_products(1)
            by_head = prod[1].rearrange("p k (h d) -> p k h d", d=DP)
            nc.gpsimd.tensor_tensor(by_head[:, :, :, 0:DP // 2], by_head[:, :, :, 0:DP // 2], by_head[:, :, :, DP // 2:], ALU.add
                                    ).then_inc(S["halved_ok"], 1)
            pool.wait_ge(S["halved_ok"], 1)

            def low_weights(raw, high_ok, low_ok):
                pool.wait_ge(S[high_ok], 1)
                nc.gpsimd.tensor_tensor(w_part[1][:], raw[:], w_part[0][:].bitcast(F32), ALU.subtract).then_inc(S[low_ok], 1)
                pool.wait_ge(S[low_ok], 1)

            pool.wait_ge(S["wb_hi"], 1)
            nc.gpsimd.tensor_tensor(wb_part[1][:], wb_b[0:1], wb_part[0][:].bitcast(F32), ALU.subtract).then_inc(S["wb_lo"], 1)
            pool.wait_ge(S["wb_lo"], 1)
            low_weights(ws_s, "ws_hi", "ws_lo")
            middle_part(3)
            for h in range(H):
                pool.wait_ge(S["relu4_ok"], h + 1)
                pool.wait_ge(S["steep_dve"], h + 1)
                nc.gpsimd.tensor_tensor(term[h % ZB], term[h % ZB], z_s[h % ZB], ALU.add).then_inc(S["leaky_ok"], 1)
                pool.wait_ge(S["leaky_ok"], h + 1)
            pool.wait_ge(S["termT_pe"], H)
            pool.wait_ge(S["wl_hi"], KT)
            nc.gpsimd.tensor_tensor(wl_part[1][:], wl_s[:], wl_part[0][:].bitcast(F32), ALU.subtract).then_inc(S["wl_lo"], 1)
            pool.wait_ge(S["wl_lo"], 1)
            low_weights(wr_s, "wr_hi", "wr_lo")
            middle_part(4)
            for t, name in enumerate(("ln2_h_act", "ln2_h_dve")):
                pool.wait_ge(S[name], 1)
                if t:
                    pool.wait_ge(S["x2_beta"], t)
                nc.gpsimd.tensor_tensor(xs[2][:, t, :], xs[2][:, t, :], beta_b, ALU.add).then_inc(S["x2_beta"], 1)
            low_weights(w3_s, "w3_hi", "w3_lo")

        @block.scalar
        def _(act):
            def layernorm_act(layer):
                act.wait_ge(S[f"ln{layer}_mv"], NT)
                nc.scalar.activation(sd[:, layer, :], bmv[:, layer, :, 1], ACT.Sqrt, bias=eps_s[:, 0:1]).then_inc(S[f"ln{layer}_sd"], 1)
                act.wait_ge(S[f"ln{layer}_nmr"], 1)
                nc.scalar.activation(hs[layer][:, 0, :], xs[layer][:, 0, :], ACT.Relu, bias=nmr[:, layer, 0:1],
                                     scale=rs[:, layer, 0:1]).then_inc(S[f"ln{layer}_h_act"], 1)

            def weight_low(c):
                a, b = CHUNKS[c]
                act.wait_ge(S["hot_ok"], 2 * c + 2)
                for g in range(a, b):
                    for i in range(2):
                        last = nc.scalar.activation(src_w[2][:, g, :, i], src_hot[:, g, :, i], ACT.Copy,
                                                    scale=ew_lo32[:, 2 * g + i:2 * g + i + 1])
                last.then_inc(S["srcw2_ok"], 1)

            act.wait_ge(S["zero_ok"], 1)
            nc.scalar.activation(warm[:], eps_s[:], ACT.Sqrt).then_inc(S["warm_ok"], 1)
            act.wait_ge(S["ew_ok"], 3)
            for t in range(NT):
                act.wait_ge(S[f"ld_x{t}"], 16)
                nc.scalar.activation(hs[0][:, t, :], xs[0][:, t, :], ACT.Identity, accum_out=sum0[:, t:t + 1]).then_inc(S["sum0_ok"], 1)
            act.wait_ge(S["sum0_ok"], NT)
            nc.scalar.mul(nmean0[:], sum0[:], -1.0 / D).then_inc(S["nmean0_ok"], 1)
            act.wait_ge(S["nmean0_ok"], 1)
            for t in range(NT):
                nc.scalar.activation(hs[0][:, t, :], xs[0][:, t, :], ACT.Square, bias=nmean0[:, t:t + 1],
                                     accum_out=sq0[:, t:t + 1]).then_inc(S["sq0_ok"], 1)
            act.wait_ge(S["sq0_ok"], NT)
            nc.scalar.activation(sd[:, 0, :], sq0[:], ACT.Sqrt, bias=eps_s[:, 0:1], scale=1.0 / D).then_inc(S["ln0_sd"], 1)
            weight_low(0)
            act.wait_ge(S["ln0_nmr"], 1)
            for t, name in enumerate(("ln0_h_act", "ln0_h_dve")):
                nc.scalar.activation(hs[0][:, t, :], xs[0][:, t, :], ACT.Relu, bias=nmr[:, 0, t:t + 1],
                                     scale=rs[:, 0, t:t + 1]).then_inc(S[name], 1)
            act.wait_ge(S["ld_w0"], 16)
            nc.scalar.copy(w_part[0][:], w0_s[:]).then_inc(S["w0_hi"], 1)
            for j in range(2):
                act.wait_ge(S["h0T_pe"], j + 1)
                nc.scalar.copy(xT_part[0][:, 2 * j:2 * j + 2, :], halves(4 + j)).then_inc(S["h0T_hi"], 1)
            for t in range(NT):
                act.wait_ge(S["counts_pe"], t + 1)
                nc.scalar.copy(cnt[:, t, :], bank[t][:, 0:N]).then_inc(S["cnt_act"], 1)
            act.wait_ge(S["ld_rows"], 16)
            act.wait_ge(S["eye_ok"], 1)
            for j in (2, 1):
                nc.scalar.activation(eye_w[j], eye[:], ACT.Copy, scale=dw_b[:, j:j + 1]).then_inc(S["eye_w_ok"], 1)
            for c in range(1, 4):
                weight_low(c)
            act.wait_ge(S["ld_rows"], 16)
            nc.scalar.copy(wb_part[0][:], wb_b[0:1]).then_inc(S["wb_hi"], 1)
            act.wait_ge(S["ld_ws"], 16)
            act.wait_ge(S["hw_pe"], NT)
            nc.scalar.copy(w_part[0][:], ws_s[:]).then_inc(S["ws_hi"], 1)
            act.wait_ge(S["dinv_ok"], 1)
            for t in range(NT):
                act.wait_ge(S["mix_pe"], t + 1)
                nc.scalar.activation(xs[1][:, t, :], bank[MIX + t][:], ACT.Relu, scale=dinv[:, t:t + 1]).then_inc(S["mixrelu_ok"], 1)
            layernorm_act(1)
            for j in range(2):
                act.wait_ge(S["h1T_pe"], j + 1)
                nc.scalar.activation(xT_part[0][:, 2 * j:2 * j + 2, :], halves(4 + j), ACT.Relu).then_inc(S["h1T_hi"], 1)
            nc.scalar.activation(warm[:], eps_s[:], ACT.Exp).then_inc(S["warm_ok"], 1)
            act.wait_ge(S["tuT_pe"], 1)
            nc.scalar.copy(tuT[0][:], bank[3][0:2 * H, 0:N]).then_inc(S["tuT_ok"], 1)

            def steep_side(h):
                act.wait_ge(S["zmax_ok"], NT * h + 1)
                if h >= ZB:
                    act.wait_ge(S["termT_pe"], h - ZB + 1)
                nc.scalar.activation(term[h % ZB][:, 0, :], z_s[h % ZB][:, 0, :], ACT.Relu, bias=t4[:, 0, h:h + 1],
                                     scale=STEEP).then_inc(S["relu4_ok"], 1)

            def exponentials(h):
                act.wait_ge(S["leaky_ok"], h + 1)
                act.wait_ge(S["shift_ok"], h // 2 + 1)
                act.wait_ge(S["shift1_ok"], h // 2 + 1)
                for dt in range(NT):
                    last = nc.scalar.activation(term[h % ZB][:, dt, :], term[h % ZB][:, dt, :], ACT.Exp, bias=shift[:, dt, h:h + 1],
                                                scale=SLOPE)
                last.then_inc(S["exp_ok"], 1)

            def sources_first(h):
                act.wait_ge(S["termT_pe"], h + 1)
                nc.scalar.copy(probs[:, h], halves(TB[h % len(TB)])).then_inc(S["probs_act"], 1)

            def split_wl(a, b):
                act.wait_ge(S["leaky_ok"], H)
                act.wait_ge(S["ld_wl"], 16)
                for k in range(a, b):
                    nc.scalar.copy(wl_part[0][:, k], wl_s[:, k]).then_inc(S["wl_hi"], 1)

            act.wait_ge(S["t4_ok"], 1)
            steep_side(0)
            steep_side(1)
            def project_1_out(t):
                act.wait_ge(S["wx_pe"], t + 1)
                nc.scalar.copy(wx[:, t].rearrange("p h d -> p (h d)"), bank[6 + t][:]).then_inc(S["wx_ok"], 1)

            for h in range(H):
                if h + 2 < H:
                    steep_side(h + 2)
                exponentials(h)
                if h < NT:
                    project_1_out(h)
                if h == H - 1:
                    split_wl(0, 2)
                if h and h - 1 not in BY_DVE:
                    sources_first(h - 1)
            split_wl(2, 3)
            sources_first(H - 1)
            split_wl(3, KT)
            nc.scalar.activation(warm[:], eps_s[:], ACT.Sqrt).then_inc(S["warm_ok"], 1)
            act.wait_ge(S["ld_wr"], 16)
            act.wait_ge(S["wx_pe"], NT)
            nc.scalar.copy(w_part[0][:], wr_s[:]).then_inc(S["wr_hi"], 1)
            layernorm_act(2)
            for j in range(2):
                act.wait_ge(S["h2T_pe"], j + 1)
                nc.scalar.copy(xT_part[0][:, 2 * j:2 * j + 2, :], halves(4 + j)).then_inc(S["h2T_hi"], 1)
            for j in range(2):
                act.wait_ge(S["agg2_pe"], j + 1)
                nc.scalar.copy(agg2T_part[0][:, 2 * j:2 * j + 2, :], halves(j)).then_inc(S["agg2_hi"], 1)
            weight_low(4)
            for m in range(KT):
                act.wait_ge(S["l2_pe"], m + 1)
                nc.scalar.activation(r_s[:, m, :], bank[4 + m][:, 0:N], ACT.Relu,
                                     bias=cols_s[:, CGB + m:CGB + m + 1]).then_inc(S["relu_ok"], 1)
                act.wait_ge(S["bn_ok"], m + 1)
                nc.scalar.activation(bn_sd[:, m:m + 1], bn2[:, m, 1:2], ACT.Sqrt, bias=eps_s[:, 0:1]).then_inc(S["bnsd_ok"], 1)
            act.wait_ge(S["ld_w3"], 16)
            act.wait_ge(S["l2r_pe"], 1)
            nc.scalar.copy(w_part[0][:], w3_s[:]).then_inc(S["w3_hi"], 1)
            layernorm_act(3)
            act.wait_ge(S["weighed_pe"], 1)
            nc.scalar.copy(weighted_T[:], halves(2)).then_inc(S["wT_ok"], 1)
            for j in range(2):
                act.wait_ge(S["agg3_pe"], j + 1)
                nc.scalar.copy(xT_part[0][:, 2 * j:2 * j + 2, :], halves(4 + j)).then_inc(S["agg3_hi"], 1)

        @block.vector
        def _(dve):
            own = [0]

            def then(ins):
                own[0] += 1
                ins.then_inc(S["dve_own"], 1)
                dve.wait_ge(S["dve_own"], own[0])

            def layernorm_stats(layer, ready):
                for t in range(NT):
                    ready(t)
                    then(nc.vector.bn_stats(bst[:, layer, t, :], xs[layer][:, t, :]))
                    nc.vector.bn_aggr(bmv[:, layer, t, :], bst[:, layer, t, :]).then_inc(S[f"ln{layer}_mv"], 1)

            def layernorm_apply(layer, relu=True):
                dve.wait_ge(S[f"ln{layer}_sd"], 1)
                then(nc.vector.reciprocal(rs[:, layer, :], sd[:, layer, :]))
                nc.vector.scalar_tensor_tensor(out=nmr[:, layer, :], in0=bmv[:, layer, :, 0], scalar=-1.0, in1=rs[:, layer, :],
                                               op0=ALU.mult, op1=ALU.mult).then_inc(S[f"ln{layer}_nmr"], 1)
                shifted = nc.vector.tensor_scalar(hs[layer][:, 1, :], xs[layer][:, 1, :], bmv[:, layer, 1, 0:1], rs[:, layer, 1:2],
                                                  ALU.subtract, ALU.mult)
                if not relu:
                    shifted.then_inc(S[f"ln{layer}_h_dve"], 1)
                    return
                then(shifted)
                nc.vector.tensor_scalar(hs[layer][:, 1, :], hs[layer][:, 1, :], 0.0, None, ALU.max).then_inc(S[f"ln{layer}_h_dve"], 1)

            def one_hot(hot, which, c):
                a, b = CHUNKS[c]
                idx = edges_bf[:, which, 2 * a:2 * b].rearrange("p (g i) -> p g i", i=2)
                nc.vector.tensor_tensor(hot[:, a:b], idx.unsqueeze(2).broadcast_to([P, b - a, N, 2]),
                                        node_id[:].unsqueeze(1).broadcast_to([P, b - a, N, 2]), ALU.is_equal).then_inc(S["hot_ok"], 1)

            def weight_high(c):
                a, b = CHUNKS[c]
                if c + 1 < len(CHUNKS):
                    dve.wait_ge(S["counted"], c + 1)
                else:
                    dve.wait_ge(S["counts_pe"], NT)
                dve.wait_ge(S["srcw1_ok"], c + 1)
                dve.wait_ge(S["srcw2_ok"], c + 1)
                part = ew_part[:, 0, 2 * a:2 * b].rearrange("p (g i) -> p g i", i=2)
                nc.vector.tensor_tensor(src_w[0][:, a:b], src_hot[:, a:b], part.unsqueeze(2).broadcast_to([P, b - a, N, 2]),
                                        ALU.mult).then_inc(S["srcw0_ok"], 1)

            nc.vector.memset(zeros[:], 0.0).then_inc(S["zeros_ok"], 1)
            dve.wait_ge(S["ld_edges"], 16)
            then(nc.vector.tensor_copy(edges_bf[:], edges_i[:]))
            dve.wait_ge(S["node_ids"], 1)
            for c in range(len(CHUNKS)):
                one_hot(dst_hot, 1, c)
                one_hot(src_hot, 0, c)
                if c == 2:
                    dve.wait_ge(S["ln0_sd"], 1)
                    then(nc.vector.reciprocal(rs[:, 0, :], sd[:, 0, :]))
                    nc.vector.tensor_tensor(nmr[:, 0, :], nmean0[:], rs[:, 0, :], ALU.mult).then_inc(S["ln0_nmr"], 1)
            dve.wait_ge(S["w0_hi"], 1)
            nc.vector.tensor_tensor(w_part[1][:], w0_s[:], w_part[0][:].bitcast(F32), ALU.subtract).then_inc(S["w0_lo"], 1)
            for j in range(2):
                dve.wait_ge(S["h0T_hi"], j + 1)
                nc.vector.tensor_tensor(xT_part[1][:, 2 * j:2 * j + 2, :], halves(4 + j), xT_part[0][:, 2 * j:2 * j + 2, :].bitcast(F32),
                                        ALU.subtract).then_inc(S["h0T_lo"], 1)
            dve.wait_ge(S["ew_ok"], 1)
            weight_high(0)

            def score_vectors(j):
                if j:
                    dve.wait_ge(S["halved_ok"], 1)
                else:
                    dve.wait_ge(S["prod_ok"], 1)
                nc.vector.tensor_reduce(v_s[:, 0:KT, j, :], prod[j].rearrange("p k (h d) -> p k h d", d=DP)[:, :, :, 0:(DP, DP // 2)[j]],
                                        mybir.AxisListType.X, ALU.add).then_inc(S["v_ok"], 1)

            def score_biases(j):
                dve.wait_ge(S["prod_ok"], 2 * j + 2)
                nc.vector.tensor_reduce(v_s[:, KT, j, :], prod_b[j].rearrange("p (h d) -> p h d", d=DP),
                                        mybir.AxisListType.X, ALU.add).then_inc(S["v_ok"], 1)

            dve.wait_ge(S["cntT_pe"], 1)
            dve.wait_ge(S["cnt_act"], NT)
            dve.wait_ge(S["eye_ok"], 1)
            for t in range(NT):
                nc.vector.tensor_tensor(sym[:, t, :], cnt[:, t, :], halves(3)[:, t, :], ALU.add).then_inc(S["cntT_ok"], 1)
            for t in range(NT):
                dve.wait_ge(S["cntT_ok"], t + 1)
                nc.vector.scalar_tensor_tensor(out=sym[:, t, :], in0=sym[:, t, :], scalar=1.0, in1=eye[:, t, :], op0=ALU.min,
                                               op1=ALU.add, accum_out=rsum[:, t:t + 1]).then_inc(S["sym_ok"], 1)
            dve.wait_ge(S["sym_ok"], NT)
            dve.wait_ge(S["ld_rows"], 16)
            nc.vector.tensor_scalar(rsum[:], rsum[:], 1.0, None, ALU.max).then_inc(S["rsum_ok"], 1)
            dve.wait_ge(S["rsum_ok"], 1)
            nc.vector.reciprocal(dinv[:], rsum[:]).then_inc(S["dinv_ok"], 1)
            dve.wait_ge(S["dinv_ok"], 1)
            then(nc.vector.tensor_scalar(dinv_w3[:], dinv[:], dw_b[:, 3:4], None, ALU.mult))
            dve.wait_ge(S["eye_w_ok"], 1)
            for t in range(NT):
                nc.vector.scalar_tensor_tensor(out=poly[0][:, t, :], in0=sym[:, t, :], scalar=dinv_w3[:, t:t + 1], in1=eye_w[2][:, t, :],
                                               op0=ALU.mult, op1=ALU.add).then_inc(S["poly0_ok"], 1)
            nc.vector.tensor_scalar(rsum_w0[:], rsum[:], dw_b[:, 0:1], None, ALU.mult).then_inc(S["y2s_ok"], 1)
            for t in range(NT):
                nc.vector.tensor_scalar(cnt_T[:, t, :], halves(3)[:, t, :], 1.0, 0.0, ALU.mult, ALU.add,
                                        accum_out=deg[:, t:t + 1]).then_inc(S["cntT_ok"], 1)
            dve.wait_ge(S["cntT_ok"], 2 * NT)
            then(nc.vector.tensor_scalar(deg1[:], deg[:], 1.0, None, ALU.max))
            nc.vector.reciprocal(rdeg[:], deg1[:]).then_inc(S["rdeg_ok"], 1)
            dve.wait_ge(S["hw_pe"], 1)
            nc.vector.tensor_tensor(hwb[:, 0, :], bank[6][:], b0_b, ALU.add).then_inc(S["hwb_ok"], 1)
            dve.wait_ge(S["prod1_pe"], 1)
            dve.wait_ge(S["eye_w_ok"], 2)
            for t in range(NT):
                nc.vector.scalar_tensor_tensor(out=poly[1][:, t, :], in0=halves(4)[:, t, :], scalar=dinv[:, t:t + 1], in1=eye_w[1][:, t, :],
                                               op0=ALU.mult, op1=ALU.add).then_inc(S["poly1_ok"], 1)
            score_vectors(0)
            score_biases(0)
            dve.wait_ge(S["prod2_pe"], 1)
            dve.wait_ge(S["y2s_ok"], 1)
            for t in range(NT):
                nc.vector.scalar_tensor_tensor(out=poly[2][:, t, :], in0=eye[:, t, :], scalar=rsum_w0[:, t:t + 1], in1=halves(5)[:, t, :],
                                               op0=ALU.mult, op1=ALU.add).then_inc(S["poly2_ok"], 1)
            dve.wait_ge(S["ident_ok"], 1)
            nc.vector.tensor_copy(ident_r[:], ident[0:16, 0:16]).then_inc(S["identr_ok"], 1)
            dve.wait_ge(S["zeros_ok"], 1)
            nc.vector.tensor_scalar(ones_r[:], zeros[0:1, 0:N], 1.0, None, ALU.add).then_inc(S["ones_ok"], 1)
            dve.wait_ge(S["hw_pe"], 2)
            nc.vector.tensor_tensor(hwb[:, 1, :], bank[7][:], b0_b, ALU.add).then_inc(S["hwb_ok"], 1)
            weight_high(1)
            score_biases(1)

            def residual_0(t):
                dve.wait_ge(S["mixrelu_ok"], t + 1)
                then(nc.vector.tensor_tensor(xs[1][:, t, :], xs[1][:, t, :], xs[0][:, t, :], ALU.add))

            layernorm_stats(1, residual_0)
            layernorm_apply(1, relu=False)
            score_vectors(1)
            dve.wait_ge(S["v_ok"], 4)
            nc.vector.tensor_tensor(v_s[:, KT, 0, :], v_s[:, KT, 0, :], ab_b, ALU.add).then_inc(S["vb_ok"], 1)
            dve.wait_ge(S["vb_ok"], 1)
            v_f = v_s[:].rearrange("p k j h -> p k (j h)")
            nc.vector.tensor_copy(v_part[0][:], v_f).then_inc(S["v_hi"], 1)
            dve.wait_ge(S["v_hi"], 1)
            nc.vector.tensor_tensor(v_part[1][:], v_f, v_part[0][:].bitcast(F32), ALU.subtract).then_inc(S["v_lo"], 1)
            for j in range(2):
                dve.wait_ge(S["h1T_hi"], j + 1)
                nc.vector.scalar_tensor_tensor(out=xT_part[1][:, 2 * j:2 * j + 2, :], in0=halves(4 + j), scalar=0.0,
                                               in1=xT_part[0][:, 2 * j:2 * j + 2, :].bitcast(F32), op0=ALU.max, op1=ALU.subtract).then_inc(S["h1T_lo"], 1)
            weight_high(2)
            dve.wait_ge(S["cntT_ok"], 2 * NT)
            nc.vector.tensor_scalar(mask[:], cnt_T[:], 0.0, NO_EDGE, ALU.is_equal, ALU.mult).then_inc(S["mask_ok"], 1)
            dve.wait_ge(S["tuT_ok"], 1)
            nc.vector.tensor_tensor(tuT[1][:], bank[3][0:2 * H, 0:N], tuT[0][:].bitcast(F32), ALU.subtract).then_inc(S["tuT_lo"], 1)
            dve.wait_ge(S["rdegb_pe"], 1)
            dve.wait_ge(S["eye_w_ok"], 2)
            dve.wait_ge(S["poly2_ok"], NT)
            nc.vector.tensor_tensor(cnt_mean[:], cnt[:], bank[1][:, 0:N].unsqueeze(1).broadcast_to([P, NT, N]), ALU.mult
                                    ).then_inc(S["cntmean_ok"], 1)

            def masked_source(h, dt):
                if dt == 0:
                    dve.wait_ge(S["ub_pe"], h // 2 + 1)
                if dt == 0 and h >= ZB:
                    dve.wait_ge(S["leaky_ok"], h - ZB + 1)
                nc.vector.tensor_tensor_reduce(
                    out=z_s[h % ZB][:, dt, :], in0=halves(UB[h // 2])[:, h % 2, :], in1=mask[:, dt, :], scale=1.0, scalar=FLOOR,
                    op0=ALU.add, op1=ALU.max, accum_out=zmax[:, dt, h:h + 1]).then_inc(S["zmax_ok"], 1)

            def steep_side(h):
                if h >= ZB:
                    dve.wait_ge(S["termT_pe"], h - ZB + 1)
                dve.wait_ge(S["zmax_ok"], NT * h + NT)
                nc.vector.tensor_scalar(term[h % ZB][:, 1, :], z_s[h % ZB][:, 1, :], nt[:, h:h + 1], STEEP, ALU.max, ALU.mult
                                        ).then_inc(S["steep_dve"], 1)

            def shifts(g):
                hh = slice(2 * g, 2 * g + 2)
                t_v = tu[:, :, 0, hh]
                dve.wait_ge(S["zmax_ok"], 4 * g + 4)
                nc.vector.tensor_tensor(top[:, :, hh], t_v, zmax[:, :, hh], ALU.add).then_inc(S["top_ok"], 1)
                dve.wait_ge(S["top_ok"], g + 1)
                nc.vector.scalar_tensor_tensor(out=smax[:, :, hh], in0=top[:, :, hh], scalar=SLOPE, in1=top[:, :, hh],
                                               op0=ALU.mult, op1=ALU.max).then_inc(S["smax_ok"], 1)
                dve.wait_ge(S["smax_ok"], g + 1)
                nc.vector.tensor_tensor(shift[:, 1, hh], t_v[:, 1], smax[:, 1, hh], ALU.subtract).then_inc(S["shift1_ok"], 1)
                nc.vector.scalar_tensor_tensor(out=shift[:, 0, hh], in0=t_v[:, 0], scalar=SLOPE, in1=smax[:, 0, hh],
                                               op0=ALU.mult, op1=ALU.subtract).then_inc(S["shift_ok"], 1)

            def times_counts(h, dt):
                if dt == 0:
                    dve.wait_ge(S["exp_ok"], h + 1)
                nc.vector.tensor_tensor_reduce(
                    out=term[h % ZB][:, dt, :], in0=term[h % ZB][:, dt, :], in1=cnt_T[:, dt, :], scale=1.0, scalar=0.0,
                    op0=ALU.mult, op1=ALU.add, accum_out=den[:, dt, h:h + 1]).then_inc(S["term_ok"], 1)

            def attention_out(half):
                hh = slice(HALF * half, HALF * half + HALF)
                dve.wait_ge(S["term_ok"], NT * HALF * (half + 1))
                then(nc.vector.tensor_scalar(den[:, :, hh], den[:, :, hh], TINY, None, ALU.max))
                then(nc.vector.reciprocal(rden[:, :, hh], den[:, :, hh]))
                cols_h = slice(half * HALF * DP, (half + 1) * HALF * DP)
                for dt in range(NT):
                    dve.wait_ge(S["att_pe"], NT * half + dt + 1)
                    nc.vector.tensor_tensor(
                        xs[2][:, dt, cols_h].rearrange("p (h d) -> p h d", d=DP), bank[ATT[half][dt]][:, cols_h].rearrange("p (h d) -> p h d", d=DP),
                        rden[:, dt, hh].unsqueeze(2).broadcast_to([P, HALF, DP]), ALU.mult).then_inc(S["scaled_ok"], 1)
                for dt in range(NT):
                    dve.wait_ge(S["scaled_ok"], NT * half + dt + 1)
                    nc.vector.tensor_tensor(xs[2][:, dt, cols_h], xs[2][:, dt, cols_h], xs[1][:, dt, cols_h], ALU.add
                                            ).then_inc(S["x2_ok"], 1)

            dve.wait_ge(S["mask_ok"], 1)
            for h in range(2):
                for dt in range(NT):
                    masked_source(h, dt)
                if h == 0:
                    dve.wait_ge(S["tu_pe"], 1)
                    nc.vector.tensor_copy(tu[:].rearrange("p t j h -> p t (j h)"),
                                          bank[TU][:, 0:NT * 2 * H].rearrange("p (t c) -> p t c", t=NT)).then_inc(S["tu_ok"], 1)
                    dve.wait_ge(S["tu_ok"], 1)
                    nc.vector.tensor_scalar(t4[:], tu[:, :, 0, :], STEEP, None, ALU.mult).then_inc(S["t4_ok"], 1)
                    nc.vector.tensor_scalar(nt[:], tu[:, 1, 0, :], -1.0, None, ALU.mult).then_inc(S["nt_ok"], 1)
                    dve.wait_ge(S["nt_ok"], 1)
                steep_side(h)
            shifts(0)
            for h in range(2, HALF):
                for dt in range(NT):
                    masked_source(h, dt)
                steep_side(h)
            shifts(1)
            def sources_first(h):
                dve.wait_ge(S["termT_pe"], h + 1)
                nc.vector.tensor_copy(probs[:, h], halves(TB[h % len(TB)])).then_inc(S["probs_dve"], 1)

            for h in range(H):
                if HALF <= h + 2 < H:
                    steep_side(h + 2)
                for dt in range(NT):
                    times_counts(h, dt)
                if h < HALF:
                    for dt in range(NT):
                        masked_source(h + HALF, dt)
                    if h % 2:
                        shifts((h + HALF) // 2)
                if h - 1 in BY_DVE:
                    sources_first(h - 1)
                if h == 5:
                    weight_high(3)
            attention_out(0)
            attention_out(1)

            layernorm_stats(2, lambda t: dve.wait_ge(S["x2_ok"], NT + t + 1))
            layernorm_apply(2)
            for j in range(2):
                dve.wait_ge(S["h2T_hi"], j + 1)
                nc.vector.tensor_tensor(xT_part[1][:, 2 * j:2 * j + 2, :], halves(4 + j), xT_part[0][:, 2 * j:2 * j + 2, :].bitcast(F32),
                                        ALU.subtract).then_inc(S["h2T_lo"], 1)
            for j in range(2):
                dve.wait_ge(S["agg2_hi"], j + 1)
                nc.vector.tensor_tensor(agg2T_part[1][:, 2 * j:2 * j + 2, :], halves(j), agg2T_part[0][:, 2 * j:2 * j + 2, :].bitcast(F32),
                                        ALU.subtract).then_inc(S["agg2_lo"], 1)
            weight_high(4)

            def norm_features(m):
                dve.wait_ge(S["bnsd_ok"], m + 1)
                one = slice(m, m + 1)
                then(nc.vector.reciprocal(bn_rs[:, one], bn_sd[:, one]))
                then(nc.vector.tensor_tensor(bn_sc[:, one], bn_rs[:, one], cols_s[:, CGB + KT + m:CGB + KT + m + 1], ALU.mult))
                nc.vector.tensor_scalar(y_s[:, m, :], r_s[:, m, :], bn2[:, m, 0:1], bn_sc[:, one], ALU.subtract, ALU.mult
                                        ).then_inc(S["y_ok"], 1)

            for m in range(KT):
                dve.wait_ge(S["relu_ok"], m + 1)
                then(nc.vector.bn_stats(bn6[:, m, :], r_s[:, m, :]))
                nc.vector.bn_aggr(bn2[:, m, :], bn6[:, m, :]).then_inc(S["bn_ok"], 1)
                if m:
                    norm_features(m - 1)
            norm_features(KT - 1)

            def residual_2(t):
                dve.wait_ge(S["yT_pe"], t + 1)
                dve.wait_ge(S["x2_beta"], NT)
                then(nc.vector.tensor_tensor(xs[3][:, t, :], bank[t][:], xs[2][:, t, :], ALU.add))

            layernorm_stats(3, residual_2)
            layernorm_apply(3)
            for j in range(2):
                dve.wait_ge(S["agg3_hi"], j + 1)
                nc.vector.tensor_tensor(xT_part[1][:, 2 * j:2 * j + 2, :], halves(4 + j), xT_part[0][:, 2 * j:2 * j + 2, :].bitcast(F32),
                                        ALU.subtract).then_inc(S["agg3_lo"], 1)
            for i, (t, a, b, out_bank) in enumerate(PIECES):
                dve.wait_ge(S["l3_pe"], i + 1)
                nc.vector.tensor_tensor(xs[4][:, t, a:b], bank[out_bank][:, a:b], xs[3][:, t, a:b], ALU.add).then_inc(S["x_ok"], 1)

        @block.tensor
        def _(pe):
            def project_1(t, a, b):
                for k in range(a, b):
                    for i, (x_part, part) in enumerate(THREE):
                        last = nc.tensor.matmul(bank[6 + t][:], xT_part[x_part][:, k, t * P:(t + 1) * P], w_part[part][:, k, :],
                                                start=(k + i == 0), stop=False)
                if b == KT:
                    for part in range(2):
                        last = nc.tensor.matmul(bank[6 + t][:], ones_r[:, 0:P], wb_part[part][:], start=False, stop=(part == 1))
                    last.then_inc(S["wx_pe"], 1)

            def keep_warm(b, n):
                pe.wait_ge(S["zeros_ok"], 1)
                for _ in range(n):
                    nc.tensor.matmul(bank[b][:], zeros[:, 0:P], zeros[:], start=True, stop=True)

            def count_edges(c):
                pe.wait_ge(S["hot_ok"], 2 * c + 2)
                for g in range(*CHUNKS[c]):
                    for i in range(2):
                        for half in range(NT):
                            last = nc.tensor.matmul(bank[half][:, 0:N], src_hot[:, g, half * P:(half + 1) * P, i],
                                                    dst_hot[:, g, :, i], start=(g + i == 0), stop=(g == PAIRS - 1 and i == 1))
                            if g == PAIRS - 1 and i == 1:
                                last.then_inc(S["counts_pe"], 1)
                            elif g == CHUNKS[c][1] - 1 and i == 1 and half == NT - 1:
                                last.then_inc(S["counted"], 1)

            def weigh_edges(a, b):
                for e in range(a, b):
                    for c, (first, _) in enumerate(CHUNKS):
                        if e == a and 2 * CHUNKS[c][1] > a and 2 * first <= a or e == 2 * first:
                            for part in range(3):
                                pe.wait_ge(S[f"srcw{part}_ok"], c + 1)
                    for half in range(NT):
                        for part in range(3):
                            last = nc.tensor.matmul(halves(2)[:, half, :], dst_hot[:, e // 2, half * P:(half + 1) * P, e % 2],
                                                    src_w[part][:, e // 2, :, e % 2], start=(e + half + part == 0),
                                                    stop=(e == ET - 1 and part == 2), skip_group_check=True)
                if b == ET:
                    last.then_inc(S["weighed_pe"], 1)

            def transpose_h(layer, name):
                for t in range(NT):
                    pe.wait_ge(S[f"ln{layer}_" + ("h_act", "h_dve")[t]], 1)
                    for k in range(KT):
                        last = nc.tensor.transpose(halves(4 + k // 2)[:, k % 2, t * P:(t + 1) * P],
                                                   hs[layer][:, t, k * P:(k + 1) * P], ident[:])
                        if t == NT - 1 and k % 2:
                            last.then_inc(S[name], 1)

            def project_0(t, a, b):
                for k in range(a, b):
                    for i, (x_part, part) in enumerate(THREE):
                        last = nc.tensor.matmul(bank[6 + t][:], xT_part[x_part][:, k, t * P:(t + 1) * P], w_part[part][:, k, :],
                                                start=(k + i == 0), stop=(k == KT - 1 and i == 2))
                if b == KT:
                    last.then_inc(S["hw_pe"], 1)

            def row_of(bank_ap, col_of):
                for t in range(NT):
                    last = nc.tensor.matmul(bank_ap[:, t * P:(t + 1) * P], col_of(t).broadcast_to([P, P]), ident[:], start=True, stop=True)
                return last

            def sym_times(mat, out_halves):
                for m in range(NT):
                    for k in range(NT):
                        last = nc.tensor.matmul(out_halves[:, m, :], sym[:, k, m * P:(m + 1) * P], mat[:, k, :], start=(k == 0), stop=(k == NT - 1))
                return last

            def aggregate_T(layer, mat, banks, name):
                for k in range(KT):
                    for t in range(NT):
                        last = nc.tensor.matmul(halves(banks[k // 2])[:, k % 2, :], hs[layer][:, t, k * P:(k + 1) * P], mat[:, t, :],
                                                start=(t == 0), stop=(t == NT - 1))
                    if k % 2:
                        last.then_inc(S[name], 1)

            keep_warm(7, 6)
            count_edges(0)
            keep_warm(7, 3)
            count_edges(1)
            keep_warm(7, 5)
            count_edges(2)
            pe.wait_ge(S["ident_ok"], 1)
            transpose_h(0, "h0T_pe")
            count_edges(3)
            count_edges(4)
            pe.wait_ge(S["cnt_act"], NT)
            for a in range(NT):
                for b in range(NT):
                    last = nc.tensor.transpose(halves(3)[:, b, a * P:(a + 1) * P], cnt[:, a, b * P:(b + 1) * P], ident[:])
            last.then_inc(S["cntT_pe"], 1)
            pe.wait_ge(S["w0_lo"], 1)
            pe.wait_ge(S["h0T_lo"], 2)
            project_0(0, 0, KT)
            weigh_edges(0, 1)
            pe.wait_ge(S["poly0_ok"], NT)
            sym_times(poly[0], halves(4)).then_inc(S["prod1_pe"], 1)
            pe.wait_ge(S["rdeg_ok"], 1)
            row_of(bank[1], lambda t: rdeg[:, t:t + 1]).then_inc(S["rdegb_pe"], 1)
            project_0(1, 0, 2)
            pe.wait_ge(S["poly1_ok"], NT)
            sym_times(poly[1], halves(5)).then_inc(S["prod2_pe"], 1)
            project_0(1, 2, KT)
            pe.wait_ge(S["poly2_ok"], NT)
            for t in range(NT):
                for k in range(NT):
                    if t == 0:
                        pe.wait_ge(S["hwb_ok"], k + 1)
                    last = nc.tensor.matmul(bank[MIX + t][:], poly[2][:, k, t * P:(t + 1) * P], hwb[:, k, :], start=(k == 0), stop=(k == NT - 1))
                last.then_inc(S["mix_pe"], 1)

            weigh_edges(1, 7)

            transpose_h(1, "h1T_pe")
            weigh_edges(7, 9)
            pe.wait_ge(S["v_lo"], 1)
            for k in range(KT):
                if k % 2 == 0:
                    pe.wait_ge(S["h1T_hi"], k // 2 + 1)
                    pe.wait_ge(S["h1T_lo"], k // 2 + 1)
                for i, (x_part, part) in enumerate(THREE):
                    nc.tensor.matmul(bank[3][0:2 * H, 0:N], v_part[part][:, k], xT_part[x_part][:, k, :], start=(k + i == 0), stop=False)
            pe.wait_ge(S["ones_ok"], 1)
            for part in range(2):
                last = nc.tensor.matmul(bank[3][0:2 * H, 0:N], v_part[part][0:1, KT], ones_r[:], start=False, stop=(part == 1))
            last.then_inc(S["tuT_pe"], 1)
            pe.wait_ge(S["ws_hi"], 1)
            pe.wait_ge(S["ws_lo"], 1)
            project_1(0, 0, 2)
            pe.wait_ge(S["tuT_lo"], 1)
            pe.wait_ge(S["identr_ok"], 1)

            def source_rows(g):
                for r in range(2):
                    row = H + 2 * g + r
                    for part in range(2):
                        last = nc.tensor.matmul(halves(UB[g])[:, r, :], ident_r[:, row:row + 1].broadcast_to([16, P]), tuT[part][:],
                                                start=(part == 0), stop=(part == 1))
                last.then_inc(S["ub_pe"], 1)

            source_rows(0)
            for t in range(NT):
                for part in range(2):
                    last = nc.tensor.matmul(bank[TU][:, 2 * H * t:2 * H * (t + 1)], tuT[part][:, t * P:(t + 1) * P], ident_r[:],
                                            start=(part == 0), stop=(part == 1))
            last.then_inc(S["tu_pe"], 1)
            source_rows(1)
            pe.wait_ge(S["cntmean_ok"], 1)
            source_rows(2)
            pe.wait_ge(S["tu_ok"], 1)
            source_rows(3)

            def wait_probs(h):
                if h in BY_DVE:
                    pe.wait_ge(S["probs_dve"], sum(i <= h for i in BY_DVE))
                else:
                    pe.wait_ge(S["probs_act"], sum(i <= h for i in range(H) if i not in BY_DVE))

            def transpose_terms(h):
                pe.wait_ge(S["term_ok"], NT * h + NT)
                if h >= len(TB):
                    wait_probs(h - len(TB))
                elif h:
                    pe.wait_ge(S["wx_ok"], h)
                for dt in range(NT):
                    for st in range(NT):
                        last = nc.tensor.transpose(halves(TB[h % len(TB)])[:, st, dt * P:(dt + 1) * P], term[h % ZB][:, dt, st * P:(st + 1) * P],
                                                   ident[:])
                last.then_inc(S["termT_pe"], 1)

            def attend(h):
                wait_probs(h)
                if h == HALF:
                    pe.wait_ge(S["zmax_ok"], NT * H)
                for dt in range(NT):
                    for st in range(NT):
                        last = nc.tensor.matmul(bank[ATT[h // HALF][dt]][:, h * DP:(h + 1) * DP], probs[:, h, st, dt * P:(dt + 1) * P],
                                                wx[:, st, h, :], start=(st == 0), stop=(st == NT - 1))
                    if h % HALF == HALF - 1:
                        last.then_inc(S["att_pe"], 1)

            pe.wait_ge(S["wb_lo"], 1)
            project_1(0, 2, KT)
            project_1(1, 0, KT)
            transpose_terms(0)
            weigh_edges(9, 11)
            pe.wait_ge(S["wx_ok"], NT)
            pe.wait_ge(S["zmax_ok"], NT * HALF)
            for h in range(H):
                if h + 1 < H:
                    transpose_terms(h + 1)
                attend(h)
                if h < HALF:
                    weigh_edges(11 + h, 12 + h)

            weigh_edges(15, 22)
            transpose_h(2, "h2T_pe")
            aggregate_T(2, cnt_mean, (0, 1), "agg2_pe")
            pe.wait_ge(S["h2T_hi"], 2)
            pe.wait_ge(S["h2T_lo"], 2)
            pe.wait_ge(S["wr_hi"], 1)
            pe.wait_ge(S["wr_lo"], 1)
            for m in range(KT):
                for k in range(KT):
                    for i, (x_part, part) in enumerate(THREE):
                        last = nc.tensor.matmul(bank[4 + m][:, 0:N], w_part[part][:, k, m * P:(m + 1) * P], xT_part[x_part][:, k, :],
                                                start=(k + i == 0), stop=False)
            last.then_inc(S["l2r_pe"], 1)
            pe.wait_ge(S["agg2_lo"], 2)
            pe.wait_ge(S["wl_lo"], 1)
            for m in range(KT):
                for k in range(KT):
                    for i, (x_part, part) in enumerate(THREE):
                        last = nc.tensor.matmul(bank[4 + m][:, 0:N], wl_part[part][:, k, m * P:(m + 1) * P], agg2T_part[x_part][:, k, :],
                                                start=False, stop=(k == KT - 1 and i == 2))
                last.then_inc(S["l2_pe"], 1)
            weigh_edges(22, 26)
            for m in range(KT):
                pe.wait_ge(S["y_ok"], m + 1)
                for t in range(NT):
                    last = nc.tensor.transpose(bank[t][:, m * P:(m + 1) * P], y_s[:, m, t * P:(t + 1) * P], ident[:])
                    if m == KT - 1:
                        last.then_inc(S["yT_pe"], 1)

            weigh_edges(26, ET)
            keep_warm(3, 3)
            
            pe.wait_ge(S["wT_ok"], 1)
            pe.wait_ge(S["ln3_h_act"], 1)
            pe.wait_ge(S["ln3_h_dve"], 1)
            aggregate_T(3, weighted_T, (4, 5), "agg3_pe")
            pe.wait_ge(S["w3_hi"], 1)
            pe.wait_ge(S["w3_lo"], 1)
            for t, a, b, out_bank in PIECES:
                for k in range(KT):
                    if t == 0 and k % 2 == 0:
                        pe.wait_ge(S["agg3_hi"], k // 2 + 1)
                        pe.wait_ge(S["agg3_lo"], k // 2 + 1)
                    for i, (x_part, part) in enumerate(THREE):
                        last = nc.tensor.matmul(bank[out_bank][:, a:b], xT_part[x_part][:, k, t * P:(t + 1) * P], w_part[part][:, k, a:b],
                                                start=(k + i == 0), stop=(k == KT - 1 and i == 2))
                last.then_inc(S["l3_pe"], 1)


def kernel(x, src, dst, edge_weight, L0_gnn_W, L0_gnn_b, L0_gnn_diffusion_weights, L1_gnn_Ws, L1_gnn_Wb, L1_gnn_a_w,
           L1_gnn_a_b, L2_gnn_W_l, L2_gnn_b_l, L2_gnn_W_r, L2_gnn_gamma, L2_gnn_beta, L3_gnn_weight):
    import numpy as np
    import concourse.bacc as bacc
    from concourse.bass_utils import run_bass_kernel_spmd

    def a(v):
        return np.asarray(v)

    p, d = 128, x.shape[1]
    ws = a(L1_gnn_Ws)
    heads = ws.shape[0]
    dp = ws.shape[2]
    cols = np.concatenate([a(L2_gnn_b_l).reshape(d // p, p).T, a(L2_gnn_gamma).reshape(d // p, p).T], axis=1)
    rows = np.concatenate([a(L0_gnn_b), a(L1_gnn_Wb).reshape(-1), a(L0_gnn_diffusion_weights), a(L1_gnn_a_b),
                           a(L2_gnn_beta), a(L1_gnn_a_w).reshape(heads, 2, dp).transpose(1, 0, 2).reshape(-1)])[None, :]
    arrays = {
        "x": a(x),
        "edges": np.stack([a(src).reshape(p, -1), a(dst).reshape(p, -1)], axis=1),
        "edge_w": a(edge_weight).reshape(p, -1),
        "w0": a(L0_gnn_W),
        "ws": ws.transpose(1, 0, 2).reshape(d, heads * dp),
        "wl_T": a(L2_gnn_W_l).T, "wr_T": a(L2_gnn_W_r).T, "w3_T": a(L3_gnn_weight).T,
        "rows": rows, "cols": cols,
    }
    arrays = {f"in_{k}": np.ascontiguousarray(v) for k, v in arrays.items()}
    nc = bacc.Bacc("TRN2", target_bir_lowering=False, num_devices=1)
    ins = [nc.dram_tensor(k, v.shape, mybir.dt.from_np(v.dtype), kind="ExternalInput").ap() for k, v in arrays.items()]
    out = nc.dram_tensor("out", x.shape, F32, kind="ExternalOutput").ap()
    gnn_program(nc, *ins, out)
    done = run_bass_kernel_spmd(nc, [arrays], core_ids=[0])
    return done.results[0]["out"]
```

```python
from contextlib import ExitStack

import concourse.bass as bass
from concourse import mybir

ALU = mybir.AluOpType
ACT = mybir.ActivationFunctionType
F32 = mybir.dt.float32
BF16 = mybir.dt.bfloat16
F32R = mybir.dt.float32r
I32 = mybir.dt.int32

P = 128
EPS = 1e-5
SLOPE = 0.2
STEEP = 4.0
NO_EDGE = -1e30
FLOOR = -1e29
TINY = 1e-30


def gnn_program(nc: bass.Bass, x, edges, edge_w, w0, ws, wl_T, wr_T, w3_T, rows, cols, out):
    N, D = x.shape
    E = edge_w.shape[0] * edge_w.shape[1]
    H, DP = 8, 64
    NT = N // P
    KT = D // P
    ET = E // P
    PAIRS = ET // 2
    CHUNKS = [(0, 1), (1, 5), (5, 9), (9, 12), (12, PAIRS)]
    HALF = H // 2
    ZB = 4
    PIECES = [(0, 0, D, 6), (1, 0, D // 2, 7), (1, D // 2, D, 0)]
    CGB = 0

    with ExitStack() as ctx:
        def sb(name, shape, dt=F32, stack=ctx):
            return stack.enter_context(nc.sbuf_tensor(name, shape, dt))

        sems = {}

        def sem(name):
            sems[name] = ctx.enter_context(nc.semaphore(name))
            return sems[name]

        with ExitStack() as early:
            w0_s = sb("w_l0", [P, KT, D], stack=early)
            prod_s = sb("prod", [P, KT, D], stack=early)
            hwb = sb("hwb", [P, NT, D], stack=early)
            wx = sb("wx", [P, NT, H, DP], stack=early)
            probs = sb("probs", [P, H, NT, N], stack=early)
            mask = sb("mask", [P, NT, N], stack=early)
            cnt = sb("cnt", [P, NT, N], stack=early)
        wl_low, wl_high = (sb(f"wl_{part}", [P, KT, D], F32R) for part in ("low", "high"))
        wl_part = [wl_high, wl_low]
        agg2T_part = [sb(f"agg2T_{part}", [P, KT, N], F32R) for part in ("high", "low")]
        r_s, y_s = (sb(f"l2_{name}", [P, KT, N]) for name in ("relu", "normed"))
        h_part = [sb(f"h_{part}", [P, NT, D], F32R) for part in ("high", "low")]
        mat_part = [sb(f"mat_{part}", [P, NT, N], F32R) for part in ("high", "low")]
        edges_i = sb("edges_i", [P, 2, ET], I32)
        edges_bf = sb("edges_bf", [P, 2, ET], BF16)
        ew = sb("ew", [P, ET])
        ew_rest = sb("ew_rest", [P, ET])
        ew_part = sb("ew_part", [P, 2, ET], BF16)
        ew_lo32 = sb("ew_lo32", [P, ET])
        node_id = sb("node_id", [P, N, 2], BF16)
        src_hot = sb("src_hot", [P, PAIRS, N, 2], BF16)
        dst_hot = sb("dst_hot", [P, PAIRS, N, 2], BF16)
        src_w = [src_hot] + [sb(f"src_w{i}", [P, PAIRS, N, 2], BF16) for i in (1, 2)]

        xs = [sb(f"x{i}", [P, NT, D]) for i in range(2)]
        xs = [xs[i % 2] for i in range(5)]
        hs = [sb(f"h{i}", [P, NT, D]) for i in range(2)]
        hs = [hs[i % 2] for i in range(4)]
        ws_s, wl_s, w3_s = (sb(f"w_{n}", [P, KT, D]) for n in ("l1", "l2l", "l3"))
        wr_s = ws_s
        w_part = [sb(f"w_{part}", [P, KT, D], F32R) for part in ("high", "low")]
        xT_part = [sb(f"xT_{part}", [P, KT, N], F32R) for part in ("high", "low")]
        THREE = ((0, 0), (0, 1), (1, 0))
        rows_s = sb("rows_s", [P, rows.shape[1]])
        cols_s = sb("cols_s", [P, cols.shape[1]])
        b0_b = rows_s[:, 0:D]
        wb_b = rows_s[:, D:2 * D]
        dw_b = rows_s[:, 2 * D:2 * D + 4]
        ab_b = rows_s[:, 2 * D + 4:2 * D + 4 + H]
        beta_b = rows_s[:, 2 * D + 4 + H:3 * D + 4 + H]
        a_b = rows_s[:, 3 * D + 4 + H:5 * D + 4 + H].rearrange("p (j n) -> p j n", j=2)

        ident = sb("ident", [P, P])
        eye = sb("eye", [P, NT, N])
        eye_w = {i: probs[:, i - 1] for i in (1, 2)}
        eps_s = sb("eps_s", [P, 1])
        warm = sb("warm", [P, 1])
        prod = [prod_s[:, :, :], probs[:, 4:8].rearrange("p h t n -> p h (t n)")]
        prod_b = [hs[1][:, 0, :], mask[:].rearrange("p t n -> p (t n)")]
        v_s = sb("v_s", [P, KT + 1, 2, H])
        v_part = [sb(f"v_{part}", [P, KT + 1, 2 * H], F32R) for part in ("high", "low")]
        zeros = sb("zeros", [P, D], BF16)
        wb_part = [sb(f"wb_{part}", [1, D], F32R) for part in ("high", "low")]
        ones_r = sb("ones_r", [1, N], F32R)
        ident_r = sb("ident_r", [16, 16], F32R)

        cnt_T = sb("cnt_T", [P, NT, N])
        sym = probs[:, 2]
        poly = [probs[:, 3], wx[:].rearrange("p t h d -> p (t h d)")[:, 0:NT * N].rearrange("p (t n) -> p t n", t=NT), probs[:, 3]]
        cnt_mean = eye
        rsum = sb("rsum", [P, NT])
        dinv = sb("dinv", [P, NT])
        dinv_w3 = sb("dinv_w3", [P, NT])
        rsum_w0 = sb("rsum_w0", [P, NT])
        deg = sb("deg", [P, NT])
        deg1 = sb("deg1", [P, NT])
        rdeg = sb("rdeg", [P, NT])

        sum0 = sb("sum0", [P, NT])
        nmean0 = sb("nmean0", [P, NT])
        sq0 = sb("sq0", [P, NT])
        sum_a = sb("sum_a", [P, 4, 2])
        nmean_a = sb("nmean_a", [P, 4, 2])
        sq_a = sb("sq_a", [P, 4])
        bst = sb("bst", [P, 4, NT, 6])
        bmv = sb("bmv", [P, 4, NT, 2])
        sd = sb("sd", [P, 4, NT])
        rs = sb("rs", [P, 4, NT])
        nmr = sb("nmr", [P, 4, NT])

        tu = sb("tu", [P, NT, 2, H])
        tuT = [sb(f"tuT_{part}", [16, N], F32R) for part in ("high", "low")]
        zmax = sb("zmax", [P, NT, H])
        top = sb("top", [P, NT, H])
        smax = sb("smax", [P, NT, H])
        shift = sb("shift", [P, NT, H])
        t4 = sb("t4", [P, NT, H])
        nt = sb("nt", [P, H])
        z_s, term = ([buf[:, i].rearrange("p (t n) -> p t n", t=NT) for i in range(ZB)] for buf in (prod[0], w0_s))
        den = sb("den", [P, NT, H])
        rden = sb("rden", [P, NT, H])

        bn6 = sb("bn6", [P, KT, 6])
        bn2 = sb("bn2", [P, KT, 2])
        bn_sd = sb("bn_sd", [P, KT])
        bn_rs = sb("bn_rs", [P, KT])
        bn_sc = sb("bn_sc", [P, KT])

        bank = [ctx.enter_context(nc.psum_tensor(f"bank{i}", [P, 512], F32)) for i in range(8)]

        def halves(b):
            return bank[b][:, :].rearrange("p (a n) -> p a n", a=2)

        UB = (4, 5, 1, 0)
        TU = 0
        MIX = 4
        ATT = ((4, 5), (0, 1))
        BY_DVE = (5,)
        TB = (3, 6, 7)

        for name in ("ld_edges", "ld_ew", "ld_x0", "ld_x1", "ld_w0", "ld_ws", "ld_wl", "ld_wr", "ld_w3", "ld_rows",
                     "ld_cols", "node_ids", "ident_ok", "eye_ok", "eye_w_ok", "x2_beta", "identr_ok", "prod_ok",
                     "halved_ok", "zero_ok", "ew_ok", "hot_ok", "srcw0_ok", "counted", "srcw1_ok", "srcw2_ok",
                     "counts_pe", "cnt_act", "cntT_pe", "cntT_ok", "sym_ok", "dinv_ok", "rsum_ok", "y2s_ok", "poly0_ok",
                     "prod1_pe", "poly1_ok", "prod2_pe", "poly2_ok", "mask_ok", "rdeg_ok", "rdegb_pe", "cntmean_ok",
                     "h0T_pe", "h0T_hi", "h0T_lo", "hw_pe", "hwb_ok", "mix_pe", "mixrelu_ok", "sum0_ok", "nmean0_ok",
                     "sq0_ok", "v_ok", "vb_ok", "h1T_pe", "h1T_hi", "h1T_lo", "ws_hi", "ws_lo", "wr_hi", "wr_lo",
                     "w3_hi", "w3_lo", "l2r_pe", "v_hi", "v_lo", "tu_pe", "tu_ok", "tuT_pe", "tuT_ok", "tuT_lo",
                     "ones_ok", "wb_hi", "wb_lo", "w0_hi", "w0_lo", "zeros_ok", "ub_pe", "zmax_ok", "top_ok", "smax_ok",
                     "shift_ok", "wx_pe", "wx_ok", "relu4_ok", "steep_dve", "nt_ok", "shift1_ok", "t4_ok", "leaky_ok",
                     "exp_ok", "term_ok", "termT_pe", "probs_act", "probs_dve", "att_pe", "scaled_ok", "x2_ok", "h2T_pe",
                     "h2T_hi", "h2T_lo", "agg2_pe", "agg2_hi", "agg2_lo", "wl_hi", "wl_lo", "l2_pe", "relu_ok", "bn_ok",
                     "bnsd_ok", "y_ok", "yT_pe", "weighed_pe", "mat_hi", "mat_lo", "h_hi0", "h_hi1", "h_lo", "agg3_pe",
                     "agg3_hi", "agg3_lo", "l3_pe", "x_ok", "warm_ok", "stored", "dve_own", "pool_own"):
            sem(name)
        for layer in range(4):
            for name in ("sd", "nmr", "h_act", "h_dve") + (("mv",) if layer else ()) + (("sum", "nmean", "sq") if layer else ()):
                sem(f"ln{layer}_{name}")
        S = sems

        block = ctx.enter_context(nc.Block())

        @block.sync
        def _(sp):
            sp.dma_start(edges_i[:], edges).then_inc(S["ld_edges"], 16)
            sp.dma_start(ew[:], edge_w).then_inc(S["ld_ew"], 16)
            sp.dma_start(xs[0][:, 0, :], x[0:P, :]).then_inc(S["ld_x0"], 16)
            sp.dma_start(xs[0][:, 1, :], x[P:N, :]).then_inc(S["ld_x1"], 16)
            sp.dma_start(w0_s[:], w0.rearrange("(k p) n -> p k n", p=P)).then_inc(S["ld_w0"], 16)
            sp.dma_start(rows_s[:], rows.broadcast_to([P, rows.shape[1]])).then_inc(S["ld_rows"], 16)
            sp.dma_start(cols_s[:], cols).then_inc(S["ld_cols"], 16)
            for dst, src, name in ((ws_s, ws, "ld_ws"), (wl_s, wl_T, "ld_wl"), (w3_s, w3_T, "ld_w3"), (wr_s, wr_T, "ld_wr")):
                if name == "ld_wr":
                    sp.wait_ge(S["ws_lo"], 1)
                sp.dma_start(dst[:], src.rearrange("(k p) n -> p k n", p=P)).then_inc(S[name], 16)
            for i, (t, a, b, _) in enumerate(PIECES):
                sp.wait_ge(S["x_ok"], i + 1)
                sp.dma_start(out[t * P:(t + 1) * P, a:b], xs[4][:, t, a:b]).then_inc(S["stored"], 16)
            sp.wait_ge(S["stored"], 16 * len(PIECES))

        @block.gpsimd
        def _(pool):
            nc.gpsimd.memset(eps_s[:], EPS).then_inc(S["zero_ok"], 1)
            nc.gpsimd.iota(node_id[:], pattern=[[1, N], [0, 2]], base=0, channel_multiplier=0,
                           allow_small_or_imprecise_dtypes=True).then_inc(S["node_ids"], 1)
            nc.gpsimd.memset(ident[:], 0.0).then_inc(S["pool_own"], 1)
            nc.gpsimd.memset(eye[:], 0.0).then_inc(S["pool_own"], 1)
            pool.wait_ge(S["pool_own"], 2)
            pool.wait_ge(S["ld_ew"], 16)
            nc.gpsimd.tensor_copy(ew_part[:, 0, :], ew[:]).then_inc(S["ew_ok"], 1)
            pool.wait_ge(S["ew_ok"], 1)
            nc.gpsimd.tensor_tensor(ew_rest[:], ew[:], ew_part[:, 0, :], ALU.subtract).then_inc(S["pool_own"], 1)
            pool.wait_ge(S["pool_own"], 3)
            nc.gpsimd.tensor_copy(ew_part[:, 1, :], ew_rest[:]).then_inc(S["ew_ok"], 1)
            pool.wait_ge(S["ew_ok"], 2)
            nc.gpsimd.tensor_tensor(ew_lo32[:], ew_rest[:], ew_part[:, 1, :], ALU.subtract).then_inc(S["ew_ok"], 1)
            pool.wait_ge(S["ew_ok"], 3)
            nc.gpsimd.affine_select(out=ident[:], in_=ident[:], compare_op=ALU.not_equal, fill=1.0, base=0,
                                    pattern=[[-1, P]], channel_multiplier=1).then_inc(S["ident_ok"], 1)
            pool.wait_ge(S["ident_ok"], 1)
            nc.gpsimd.affine_select(out=eye[:], in_=eye[:], compare_op=ALU.not_equal, fill=1.0, base=0,
                                    pattern=[[P, NT], [-1, N]], channel_multiplier=1).then_inc(S["eye_ok"], 1)
            pool.wait_ge(S["eye_ok"], 1)

            def middle_part(c):
                a, b = CHUNKS[c]
                pool.wait_ge(S["hot_ok"], 2 * c + 2)
                nc.gpsimd.tensor_tensor(
                    src_w[1][:, a:b], src_hot[:, a:b],
                    ew_part[:, 1, 2 * a:2 * b].rearrange("p (g i) -> p g i", i=2).unsqueeze(2).broadcast_to([P, b - a, N, 2]),
                    ALU.mult).then_inc(S["srcw1_ok"], 1)
                pool.wait_ge(S["srcw1_ok"], c + 1)

            def score_products(j):
                nc.gpsimd.tensor_tensor(prod[j], ws_s[:], a_b[:, j].unsqueeze(1).broadcast_to([P, KT, D]), ALU.mult
                                        ).then_inc(S["prod_ok"], 1)
                pool.wait_ge(S["prod_ok"], 2 * j + 1)
                nc.gpsimd.tensor_tensor(prod_b[j], wb_b, a_b[:, j], ALU.mult).then_inc(S["prod_ok"], 1)
                pool.wait_ge(S["prod_ok"], 2 * j + 2)

            for c in range(3):
                middle_part(c)
            pool.wait_ge(S["ld_rows"], 16)
            pool.wait_ge(S["ld_ws"], 16)
            score_products(0)
            score_products(1)
            by_head = prod[1].rearrange("p k (h d) -> p k h d", d=DP)
            nc.gpsimd.tensor_tensor(by_head[:, :, :, 0:DP // 2], by_head[:, :, :, 0:DP // 2], by_head[:, :, :, DP // 2:], ALU.add
                                    ).then_inc(S["halved_ok"], 1)
            pool.wait_ge(S["halved_ok"], 1)

            def low_weights(raw, high_ok, low_ok, steps=1):
                pool.wait_ge(S[high_ok], steps)
                nc.gpsimd.tensor_tensor(w_part[1][:], raw[:], w_part[0][:].bitcast(F32), ALU.subtract).then_inc(S[low_ok], 1)
                pool.wait_ge(S[low_ok], 1)

            pool.wait_ge(S["wb_hi"], 1)
            nc.gpsimd.tensor_tensor(wb_part[1][:], wb_b[0:1], wb_part[0][:].bitcast(F32), ALU.subtract).then_inc(S["wb_lo"], 1)
            pool.wait_ge(S["wb_lo"], 1)
            low_weights(ws_s, "ws_hi", "ws_lo")
            middle_part(3)
            middle_part(4)
            for h in range(H):
                pool.wait_ge(S["relu4_ok"], h + 1)
                pool.wait_ge(S["steep_dve"], h + 1)
                nc.gpsimd.tensor_tensor(term[h % ZB], term[h % ZB], z_s[h % ZB], ALU.add).then_inc(S["leaky_ok"], 1)
                pool.wait_ge(S["leaky_ok"], h + 1)
            pool.wait_ge(S["mat_hi"], 1)
            nc.gpsimd.tensor_tensor(mat_part[1][:], cnt_mean[:], mat_part[0][:].bitcast(F32), ALU.subtract).then_inc(S["mat_lo"], 1)
            pool.wait_ge(S["mat_lo"], 1)
            low_weights(wr_s, "wr_hi", "wr_lo", KT)
            pool.wait_ge(S["termT_pe"], H)
            pool.wait_ge(S["wl_hi"], KT)
            nc.gpsimd.tensor_tensor(wl_part[1][:], wl_s[:], wl_part[0][:].bitcast(F32), ALU.subtract).then_inc(S["wl_lo"], 1)
            pool.wait_ge(S["wl_lo"], 1)
            for t, name in enumerate(("ln2_h_act", "ln2_h_dve")):
                pool.wait_ge(S[name], 1)
                if t:
                    pool.wait_ge(S["x2_beta"], t)
                nc.gpsimd.tensor_tensor(xs[2][:, t, :], xs[2][:, t, :], beta_b, ALU.add).then_inc(S["x2_beta"], 1)
            low_weights(w3_s, "w3_hi", "w3_lo")

        @block.scalar
        def _(act):
            def first_deviation(layer, halves_of_columns=1):
                for i in range(halves_of_columns):
                    act.wait_ge(S[f"ln{layer}_sum"], i + 1)
                    if i:
                        act.wait_ge(S[f"ln{layer}_nmean"], i)
                    nc.scalar.activation(nmean_a[:, layer, i:i + 1], sum_a[:, layer, i:i + 1], ACT.Identity, scale=-1.0 / D,
                                         bias=nmean_a[:, layer, i - 1:i] if i else 0.0).then_inc(S[f"ln{layer}_nmean"], 1)
                act.wait_ge(S[f"ln{layer}_nmean"], halves_of_columns)
                nc.scalar.activation(hs[layer][:, 0, :], xs[layer][:, 0, :], ACT.Square, bias=nmean_a[:, layer, i:i + 1],
                                     accum_out=sq_a[:, layer:layer + 1]).then_inc(S[f"ln{layer}_sq"], 1)
                act.wait_ge(S[f"ln{layer}_sq"], 1)
                nc.scalar.activation(sd[:, layer, 0:1], sq_a[:, layer:layer + 1], ACT.Sqrt, bias=eps_s[:, 0:1], scale=1.0 / D
                                     ).then_inc(S[f"ln{layer}_sd"], 1)

            def layernorm_act(layer):
                act.wait_ge(S[f"ln{layer}_mv"], 1)
                nc.scalar.activation(sd[:, layer, 1:2], bmv[:, layer, 1, 1:2], ACT.Sqrt, bias=eps_s[:, 0:1]).then_inc(S[f"ln{layer}_sd"], 1)
                act.wait_ge(S[f"ln{layer}_nmr"], 1)
                nc.scalar.activation(hs[layer][:, 0, :], xs[layer][:, 0, :], ACT.Relu, bias=nmr[:, layer, 0:1],
                                     scale=rs[:, layer, 0:1]).then_inc(S[f"ln{layer}_h_act"], 1)

            def split_h(layer):
                act.wait_ge(S[f"ln{layer}_h_act"], 1)
                nc.scalar.copy(h_part[0][:, 0, :], hs[layer][:, 0, :]).then_inc(S["h_hi0"], 1)

            def weight_low(c):
                a, b = CHUNKS[c]
                act.wait_ge(S["hot_ok"], 2 * c + 2)
                for g in range(a, b):
                    for i in range(2):
                        last = nc.scalar.activation(src_w[2][:, g, :, i], src_hot[:, g, :, i], ACT.Copy,
                                                    scale=ew_lo32[:, 2 * g + i:2 * g + i + 1])
                last.then_inc(S["srcw2_ok"], 1)

            act.wait_ge(S["zero_ok"], 1)
            nc.scalar.activation(warm[:], eps_s[:], ACT.Sqrt).then_inc(S["warm_ok"], 1)
            act.wait_ge(S["ew_ok"], 3)
            for t in range(NT):
                act.wait_ge(S[f"ld_x{t}"], 16)
                nc.scalar.activation(hs[0][:, t, :], xs[0][:, t, :], ACT.Identity, accum_out=sum0[:, t:t + 1]).then_inc(S["sum0_ok"], 1)
            act.wait_ge(S["sum0_ok"], NT)
            nc.scalar.mul(nmean0[:], sum0[:], -1.0 / D).then_inc(S["nmean0_ok"], 1)
            act.wait_ge(S["nmean0_ok"], 1)
            for t in range(NT):
                nc.scalar.activation(hs[0][:, t, :], xs[0][:, t, :], ACT.Square, bias=nmean0[:, t:t + 1],
                                     accum_out=sq0[:, t:t + 1]).then_inc(S["sq0_ok"], 1)
            act.wait_ge(S["sq0_ok"], NT)
            nc.scalar.activation(sd[:, 0, :], sq0[:], ACT.Sqrt, bias=eps_s[:, 0:1], scale=1.0 / D).then_inc(S["ln0_sd"], 1)
            weight_low(0)
            act.wait_ge(S["ln0_nmr"], 1)
            for t, name in enumerate(("ln0_h_act", "ln0_h_dve")):
                nc.scalar.activation(hs[0][:, t, :], xs[0][:, t, :], ACT.Relu, bias=nmr[:, 0, t:t + 1],
                                     scale=rs[:, 0, t:t + 1]).then_inc(S[name], 1)
            act.wait_ge(S["ld_w0"], 16)
            nc.scalar.copy(w_part[0][:], w0_s[:]).then_inc(S["w0_hi"], 1)
            for j in range(2):
                act.wait_ge(S["h0T_pe"], j + 1)
                nc.scalar.copy(xT_part[0][:, 2 * j:2 * j + 2, :], halves(4 + j)).then_inc(S["h0T_hi"], 1)
            for t in range(NT):
                act.wait_ge(S["counts_pe"], t + 1)
                nc.scalar.copy(cnt[:, t, :], bank[t][:, 0:N]).then_inc(S["cnt_act"], 1)
            act.wait_ge(S["ld_rows"], 16)
            act.wait_ge(S["eye_ok"], 1)
            for j in (2, 1):
                nc.scalar.activation(eye_w[j], eye[:], ACT.Copy, scale=dw_b[:, j:j + 1]).then_inc(S["eye_w_ok"], 1)
            for c in range(1, 4):
                weight_low(c)
            act.wait_ge(S["ld_rows"], 16)
            nc.scalar.copy(wb_part[0][:], wb_b[0:1]).then_inc(S["wb_hi"], 1)
            act.wait_ge(S["ld_ws"], 16)
            act.wait_ge(S["hw_pe"], NT)
            nc.scalar.copy(w_part[0][:], ws_s[:]).then_inc(S["ws_hi"], 1)
            act.wait_ge(S["dinv_ok"], 1)
            for t in range(NT):
                act.wait_ge(S["mix_pe"], t + 1)
                nc.scalar.activation(xs[1][:, t, :], bank[MIX + t][:], ACT.Relu, scale=dinv[:, t:t + 1]).then_inc(S["mixrelu_ok"], 1)
            first_deviation(1)
            layernorm_act(1)
            for j in range(2):
                act.wait_ge(S["h1T_pe"], j + 1)
                nc.scalar.activation(xT_part[0][:, 2 * j:2 * j + 2, :], halves(4 + j), ACT.Relu).then_inc(S["h1T_hi"], 1)
            nc.scalar.activation(warm[:], eps_s[:], ACT.Exp).then_inc(S["warm_ok"], 1)
            act.wait_ge(S["tuT_pe"], 1)
            nc.scalar.copy(tuT[0][:], bank[3][0:2 * H, 0:N]).then_inc(S["tuT_ok"], 1)

            def steep_side(h):
                act.wait_ge(S["zmax_ok"], NT * h + 1)
                if h >= ZB:
                    act.wait_ge(S["termT_pe"], h - ZB + 1)
                nc.scalar.activation(term[h % ZB][:, 0, :], z_s[h % ZB][:, 0, :], ACT.Relu, bias=t4[:, 0, h:h + 1],
                                     scale=STEEP).then_inc(S["relu4_ok"], 1)

            def exponentials(h):
                act.wait_ge(S["leaky_ok"], h + 1)
                act.wait_ge(S["shift_ok"], h // 2 + 1)
                act.wait_ge(S["shift1_ok"], h // 2 + 1)
                for dt in range(NT):
                    last = nc.scalar.activation(term[h % ZB][:, dt, :], term[h % ZB][:, dt, :], ACT.Exp, bias=shift[:, dt, h:h + 1],
                                                scale=SLOPE)
                last.then_inc(S["exp_ok"], 1)

            def sources_first(h):
                act.wait_ge(S["termT_pe"], h + 1)
                nc.scalar.copy(probs[:, h], halves(TB[h % len(TB)])).then_inc(S["probs_act"], 1)

            def split_wl(a, b):
                act.wait_ge(S["leaky_ok"], H)
                act.wait_ge(S["ld_wl"], 16)
                for k in range(a, b):
                    nc.scalar.copy(wl_part[0][:, k], wl_s[:, k]).then_inc(S["wl_hi"], 1)

            def split_wr(a, b):
                act.wait_ge(S["ld_wr"], 16)
                act.wait_ge(S["wx_pe"], NT)
                for k in range(a, b):
                    nc.scalar.copy(w_part[0][:, k], wr_s[:, k]).then_inc(S["wr_hi"], 1)

            act.wait_ge(S["t4_ok"], 1)
            steep_side(0)
            steep_side(1)
            def project_1_out(t):
                act.wait_ge(S["wx_pe"], t + 1)
                nc.scalar.copy(wx[:, t].rearrange("p h d -> p (h d)"), bank[6 + t][:]).then_inc(S["wx_ok"], 1)

            for h in range(H):
                if h + 2 < H:
                    steep_side(h + 2)
                exponentials(h)
                if h < NT:
                    project_1_out(h)
                if h == H - 1:
                    act.wait_ge(S["zmax_ok"], NT * H)
                    act.wait_ge(S["cntmean_ok"], 1)
                    nc.scalar.copy(mat_part[0][:], cnt_mean[:]).then_inc(S["mat_hi"], 1)
                    split_wr(0, 2)
                if h and h - 1 not in BY_DVE:
                    sources_first(h - 1)
            split_wr(2, 3)
            sources_first(H - 1)
            nc.scalar.activation(warm[:], eps_s[:], ACT.Sqrt).then_inc(S["warm_ok"], 1)
            split_wr(3, KT)
            first_deviation(2, 2)
            layernorm_act(2)
            split_h(2)
            split_wl(0, 1)
            for j in range(2):
                act.wait_ge(S["h2T_pe"], j + 1)
                nc.scalar.copy(xT_part[0][:, 2 * j:2 * j + 2, :], halves(4 + j)).then_inc(S["h2T_hi"], 1)
            for j in range(2):
                split_wl(2 * j + 1, min(2 * j + 3, KT))
                act.wait_ge(S["agg2_pe"], j + 1)
                nc.scalar.copy(agg2T_part[0][:, 2 * j:2 * j + 2, :], halves(j)).then_inc(S["agg2_hi"], 1)
            weight_low(4)
            for m in range(KT):
                act.wait_ge(S["l2_pe"], m + 1)
                nc.scalar.activation(r_s[:, m, :], bank[4 + m][:, 0:N], ACT.Relu,
                                     bias=cols_s[:, CGB + m:CGB + m + 1]).then_inc(S["relu_ok"], 1)
                act.wait_ge(S["bn_ok"], m + 1)
                nc.scalar.activation(bn_sd[:, m:m + 1], bn2[:, m, 1:2], ACT.Sqrt, bias=eps_s[:, 0:1]).then_inc(S["bnsd_ok"], 1)
            act.wait_ge(S["ld_w3"], 16)
            act.wait_ge(S["l2r_pe"], 1)
            nc.scalar.copy(w_part[0][:], w3_s[:]).then_inc(S["w3_hi"], 1)
            first_deviation(3)
            layernorm_act(3)
            split_h(3)
            act.wait_ge(S["weighed_pe"], 1)
            nc.scalar.copy(mat_part[0][:], halves(2)).then_inc(S["mat_hi"], 1)
            for j in range(2):
                act.wait_ge(S["agg3_pe"], j + 1)
                nc.scalar.copy(xT_part[0][:, 2 * j:2 * j + 2, :], halves(4 + j)).then_inc(S["agg3_hi"], 1)

        @block.vector
        def _(dve):
            own = [0]

            def then(ins):
                own[0] += 1
                ins.then_inc(S["dve_own"], 1)
                dve.wait_ge(S["dve_own"], own[0])

            def layernorm_dve(layer, relu=True):
                then(nc.vector.bn_stats(bst[:, layer, 1, :], xs[layer][:, 1, :]))
                nc.vector.bn_aggr(bmv[:, layer, 1, :], bst[:, layer, 1, :]).then_inc(S[f"ln{layer}_mv"], 1)
                dve.wait_ge(S[f"ln{layer}_sd"], 1)
                then(nc.vector.reciprocal(rs[:, layer, 0:1], sd[:, layer, 0:1]))
                last = (None, 0, 1, 0)[layer]
                nc.vector.tensor_tensor(nmr[:, layer, 0:1], nmean_a[:, layer, last:last + 1], rs[:, layer, 0:1], ALU.mult
                                        ).then_inc(S[f"ln{layer}_nmr"], 1)
                dve.wait_ge(S[f"ln{layer}_sd"], 2)
                then(nc.vector.reciprocal(rs[:, layer, 1:2], sd[:, layer, 1:2]))
                shifted = nc.vector.tensor_scalar(hs[layer][:, 1, :], xs[layer][:, 1, :], bmv[:, layer, 1, 0:1], rs[:, layer, 1:2],
                                                  ALU.subtract, ALU.mult)
                if not relu:
                    shifted.then_inc(S[f"ln{layer}_h_dve"], 1)
                    return
                then(shifted)
                nc.vector.tensor_scalar(hs[layer][:, 1, :], hs[layer][:, 1, :], 0.0, None, ALU.max).then_inc(S[f"ln{layer}_h_dve"], 1)

            def split_h(layer):
                dve.wait_ge(S[f"ln{layer}_h_dve"], 1)
                nc.vector.tensor_scalar(h_part[0][:, 1, :], hs[layer][:, 1, :], 0.0, None, ALU.max).then_inc(S["h_hi1"], 1)
                for t in (1, 0):
                    dve.wait_ge(S[f"h_hi{t}"], layer - 1)
                    nc.vector.scalar_tensor_tensor(out=h_part[1][:, t, :], in0=hs[layer][:, t, :], scalar=0.0, in1=h_part[0][:, t, :].bitcast(F32),
                                                   op0=ALU.max, op1=ALU.subtract).then_inc(S["h_lo"], 1)

            def one_hot(hot, which, c):
                a, b = CHUNKS[c]
                idx = edges_bf[:, which, 2 * a:2 * b].rearrange("p (g i) -> p g i", i=2)
                nc.vector.tensor_tensor(hot[:, a:b], idx.unsqueeze(2).broadcast_to([P, b - a, N, 2]),
                                        node_id[:].unsqueeze(1).broadcast_to([P, b - a, N, 2]), ALU.is_equal).then_inc(S["hot_ok"], 1)

            def weight_high(c):
                a, b = CHUNKS[c]
                if c + 1 < len(CHUNKS):
                    dve.wait_ge(S["counted"], c + 1)
                else:
                    dve.wait_ge(S["counts_pe"], NT)
                dve.wait_ge(S["srcw1_ok"], c + 1)
                dve.wait_ge(S["srcw2_ok"], c + 1)
                part = ew_part[:, 0, 2 * a:2 * b].rearrange("p (g i) -> p g i", i=2)
                nc.vector.tensor_tensor(src_w[0][:, a:b], src_hot[:, a:b], part.unsqueeze(2).broadcast_to([P, b - a, N, 2]),
                                        ALU.mult).then_inc(S["srcw0_ok"], 1)

            nc.vector.memset(zeros[:], 0.0).then_inc(S["zeros_ok"], 1)
            dve.wait_ge(S["ld_edges"], 16)
            then(nc.vector.tensor_copy(edges_bf[:], edges_i[:]))
            dve.wait_ge(S["node_ids"], 1)
            for c in range(len(CHUNKS)):
                one_hot(dst_hot, 1, c)
                one_hot(src_hot, 0, c)
                if c == 2:
                    dve.wait_ge(S["ln0_sd"], 1)
                    then(nc.vector.reciprocal(rs[:, 0, :], sd[:, 0, :]))
                    nc.vector.tensor_tensor(nmr[:, 0, :], nmean0[:], rs[:, 0, :], ALU.mult).then_inc(S["ln0_nmr"], 1)
            dve.wait_ge(S["w0_hi"], 1)
            nc.vector.tensor_tensor(w_part[1][:], w0_s[:], w_part[0][:].bitcast(F32), ALU.subtract).then_inc(S["w0_lo"], 1)
            dve.wait_ge(S["ew_ok"], 1)
            weight_high(0)
            for j in range(2):
                dve.wait_ge(S["h0T_hi"], j + 1)
                nc.vector.tensor_tensor(xT_part[1][:, 2 * j:2 * j + 2, :], halves(4 + j), xT_part[0][:, 2 * j:2 * j + 2, :].bitcast(F32),
                                        ALU.subtract).then_inc(S["h0T_lo"], 1)

            def score_vectors(j):
                if j:
                    dve.wait_ge(S["halved_ok"], 1)
                else:
                    dve.wait_ge(S["prod_ok"], 1)
                nc.vector.tensor_reduce(v_s[:, 0:KT, j, :], prod[j].rearrange("p k (h d) -> p k h d", d=DP)[:, :, :, 0:(DP, DP // 2)[j]],
                                        mybir.AxisListType.X, ALU.add).then_inc(S["v_ok"], 1)

            def score_biases(j):
                dve.wait_ge(S["prod_ok"], 2 * j + 2)
                nc.vector.tensor_reduce(v_s[:, KT, j, :], prod_b[j].rearrange("p (h d) -> p h d", d=DP),
                                        mybir.AxisListType.X, ALU.add).then_inc(S["v_ok"], 1)

            dve.wait_ge(S["cntT_pe"], 1)
            dve.wait_ge(S["cnt_act"], NT)
            dve.wait_ge(S["eye_ok"], 1)
            for t in range(NT):
                nc.vector.tensor_tensor(sym[:, t, :], cnt[:, t, :], halves(3)[:, t, :], ALU.add).then_inc(S["cntT_ok"], 1)
            for t in range(NT):
                dve.wait_ge(S["cntT_ok"], t + 1)
                nc.vector.scalar_tensor_tensor(out=sym[:, t, :], in0=sym[:, t, :], scalar=1.0, in1=eye[:, t, :], op0=ALU.min,
                                               op1=ALU.add, accum_out=rsum[:, t:t + 1]).then_inc(S["sym_ok"], 1)
            dve.wait_ge(S["sym_ok"], NT)
            dve.wait_ge(S["ld_rows"], 16)
            nc.vector.tensor_scalar(rsum[:], rsum[:], 1.0, None, ALU.max).then_inc(S["rsum_ok"], 1)
            dve.wait_ge(S["rsum_ok"], 1)
            nc.vector.reciprocal(dinv[:], rsum[:]).then_inc(S["dinv_ok"], 1)
            dve.wait_ge(S["dinv_ok"], 1)
            then(nc.vector.tensor_scalar(dinv_w3[:], dinv[:], dw_b[:, 3:4], None, ALU.mult))
            dve.wait_ge(S["eye_w_ok"], 1)
            for t in range(NT):
                nc.vector.scalar_tensor_tensor(out=poly[0][:, t, :], in0=sym[:, t, :], scalar=dinv_w3[:, t:t + 1], in1=eye_w[2][:, t, :],
                                               op0=ALU.mult, op1=ALU.add).then_inc(S["poly0_ok"], 1)
            nc.vector.tensor_scalar(rsum_w0[:], rsum[:], dw_b[:, 0:1], None, ALU.mult).then_inc(S["y2s_ok"], 1)
            for t in range(NT):
                nc.vector.tensor_scalar(cnt_T[:, t, :], halves(3)[:, t, :], 1.0, 0.0, ALU.mult, ALU.add,
                                        accum_out=deg[:, t:t + 1]).then_inc(S["cntT_ok"], 1)
            dve.wait_ge(S["cntT_ok"], 2 * NT)
            then(nc.vector.tensor_scalar(deg1[:], deg[:], 1.0, None, ALU.max))
            nc.vector.reciprocal(rdeg[:], deg1[:]).then_inc(S["rdeg_ok"], 1)
            dve.wait_ge(S["hw_pe"], 1)
            nc.vector.tensor_tensor(hwb[:, 0, :], bank[6][:], b0_b, ALU.add).then_inc(S["hwb_ok"], 1)
            dve.wait_ge(S["prod1_pe"], 1)
            dve.wait_ge(S["eye_w_ok"], 2)
            for t in range(NT):
                nc.vector.scalar_tensor_tensor(out=poly[1][:, t, :], in0=halves(4)[:, t, :], scalar=dinv[:, t:t + 1], in1=eye_w[1][:, t, :],
                                               op0=ALU.mult, op1=ALU.add).then_inc(S["poly1_ok"], 1)
            score_vectors(0)
            score_biases(0)
            dve.wait_ge(S["prod2_pe"], 1)
            dve.wait_ge(S["y2s_ok"], 1)
            for t in range(NT):
                nc.vector.scalar_tensor_tensor(out=poly[2][:, t, :], in0=eye[:, t, :], scalar=rsum_w0[:, t:t + 1], in1=halves(5)[:, t, :],
                                               op0=ALU.mult, op1=ALU.add).then_inc(S["poly2_ok"], 1)
            dve.wait_ge(S["ident_ok"], 1)
            nc.vector.tensor_copy(ident_r[:], ident[0:16, 0:16]).then_inc(S["identr_ok"], 1)
            dve.wait_ge(S["zeros_ok"], 1)
            nc.vector.tensor_scalar(ones_r[:], zeros[0:1, 0:N], 1.0, None, ALU.add).then_inc(S["ones_ok"], 1)
            dve.wait_ge(S["hw_pe"], 2)
            nc.vector.tensor_tensor(hwb[:, 1, :], bank[7][:], b0_b, ALU.add).then_inc(S["hwb_ok"], 1)
            weight_high(1)
            score_biases(1)

            dve.wait_ge(S["mixrelu_ok"], 1)
            nc.vector.scalar_tensor_tensor(out=xs[1][:, 0, :], in0=xs[1][:, 0, :], scalar=1.0, in1=xs[0][:, 0, :], op0=ALU.mult,
                                           op1=ALU.add, accum_out=sum_a[:, 1, 0:1]).then_inc(S["ln1_sum"], 1)
            dve.wait_ge(S["mixrelu_ok"], NT)
            then(nc.vector.tensor_tensor(xs[1][:, 1, :], xs[1][:, 1, :], xs[0][:, 1, :], ALU.add))

            layernorm_dve(1, relu=False)
            score_vectors(1)
            dve.wait_ge(S["v_ok"], 4)
            nc.vector.tensor_tensor(v_s[:, KT, 0, :], v_s[:, KT, 0, :], ab_b, ALU.add).then_inc(S["vb_ok"], 1)
            dve.wait_ge(S["vb_ok"], 1)
            v_f = v_s[:].rearrange("p k j h -> p k (j h)")
            nc.vector.tensor_copy(v_part[0][:], v_f).then_inc(S["v_hi"], 1)
            dve.wait_ge(S["v_hi"], 1)
            nc.vector.tensor_tensor(v_part[1][:], v_f, v_part[0][:].bitcast(F32), ALU.subtract).then_inc(S["v_lo"], 1)
            for j in range(2):
                dve.wait_ge(S["h1T_hi"], j + 1)
                nc.vector.scalar_tensor_tensor(out=xT_part[1][:, 2 * j:2 * j + 2, :], in0=halves(4 + j), scalar=0.0,
                                               in1=xT_part[0][:, 2 * j:2 * j + 2, :].bitcast(F32), op0=ALU.max, op1=ALU.subtract).then_inc(S["h1T_lo"], 1)
            weight_high(2)
            dve.wait_ge(S["cntT_ok"], 2 * NT)
            nc.vector.tensor_scalar(mask[:], cnt_T[:], 0.0, NO_EDGE, ALU.is_equal, ALU.mult).then_inc(S["mask_ok"], 1)
            dve.wait_ge(S["tuT_ok"], 1)
            nc.vector.tensor_tensor(tuT[1][:], bank[3][0:2 * H, 0:N], tuT[0][:].bitcast(F32), ALU.subtract).then_inc(S["tuT_lo"], 1)
            dve.wait_ge(S["rdegb_pe"], 1)
            dve.wait_ge(S["eye_w_ok"], 2)
            dve.wait_ge(S["poly2_ok"], NT)
            nc.vector.tensor_tensor(cnt_mean[:], cnt[:], bank[1][:, 0:N].unsqueeze(1).broadcast_to([P, NT, N]), ALU.mult
                                    ).then_inc(S["cntmean_ok"], 1)

            def masked_source(h, dt):
                if dt == 0:
                    dve.wait_ge(S["ub_pe"], h // 2 + 1)
                if dt == 0 and h >= ZB:
                    dve.wait_ge(S["leaky_ok"], h - ZB + 1)
                nc.vector.tensor_tensor_reduce(
                    out=z_s[h % ZB][:, dt, :], in0=halves(UB[h // 2])[:, h % 2, :], in1=mask[:, dt, :], scale=1.0, scalar=FLOOR,
                    op0=ALU.add, op1=ALU.max, accum_out=zmax[:, dt, h:h + 1]).then_inc(S["zmax_ok"], 1)

            def steep_side(h):
                if h >= ZB:
                    dve.wait_ge(S["termT_pe"], h - ZB + 1)
                dve.wait_ge(S["zmax_ok"], NT * h + NT)
                nc.vector.tensor_scalar(term[h % ZB][:, 1, :], z_s[h % ZB][:, 1, :], nt[:, h:h + 1], STEEP, ALU.max, ALU.mult
                                        ).then_inc(S["steep_dve"], 1)

            def largest_sums(g):
                hh = slice(2 * g, 2 * g + 2)
                dve.wait_ge(S["zmax_ok"], 4 * g + 4)
                nc.vector.tensor_tensor(top[:, :, hh], tu[:, :, 0, hh], zmax[:, :, hh], ALU.add).then_inc(S["top_ok"], 1)

            def largest_scores(g):
                hh = slice(2 * g, 2 * g + 2)
                dve.wait_ge(S["top_ok"], g + 1)
                nc.vector.scalar_tensor_tensor(out=smax[:, :, hh], in0=top[:, :, hh], scalar=SLOPE, in1=top[:, :, hh],
                                               op0=ALU.mult, op1=ALU.max).then_inc(S["smax_ok"], 1)

            def shifts(g):
                hh = slice(2 * g, 2 * g + 2)
                dve.wait_ge(S["smax_ok"], g + 1)
                nc.vector.tensor_tensor(shift[:, 1, hh], tu[:, 1, 0, hh], smax[:, 1, hh], ALU.subtract).then_inc(S["shift1_ok"], 1)
                nc.vector.scalar_tensor_tensor(out=shift[:, 0, hh], in0=tu[:, 0, 0, hh], scalar=SLOPE, in1=smax[:, 0, hh],
                                               op0=ALU.mult, op1=ALU.subtract).then_inc(S["shift_ok"], 1)

            def times_counts(h, dt):
                if dt == 0:
                    dve.wait_ge(S["exp_ok"], h + 1)
                nc.vector.tensor_tensor_reduce(
                    out=term[h % ZB][:, dt, :], in0=term[h % ZB][:, dt, :], in1=cnt_T[:, dt, :], scale=1.0, scalar=0.0,
                    op0=ALU.mult, op1=ALU.add, accum_out=den[:, dt, h:h + 1]).then_inc(S["term_ok"], 1)

            def attention_out(half):
                hh = slice(HALF * half, HALF * half + HALF)
                dve.wait_ge(S["term_ok"], NT * HALF * (half + 1))
                then(nc.vector.tensor_scalar(den[:, :, hh], den[:, :, hh], TINY, None, ALU.max))
                then(nc.vector.reciprocal(rden[:, :, hh], den[:, :, hh]))
                cols_h = slice(half * HALF * DP, (half + 1) * HALF * DP)
                for dt in range(NT):
                    dve.wait_ge(S["att_pe"], NT * half + dt + 1)
                    nc.vector.tensor_tensor(
                        xs[2][:, dt, cols_h].rearrange("p (h d) -> p h d", d=DP), bank[ATT[half][dt]][:, cols_h].rearrange("p (h d) -> p h d", d=DP),
                        rden[:, dt, hh].unsqueeze(2).broadcast_to([P, HALF, DP]), ALU.mult).then_inc(S["scaled_ok"], 1)
                for dt in range(NT):
                    dve.wait_ge(S["scaled_ok"], NT * half + dt + 1)
                    if dt:
                        nc.vector.tensor_tensor(xs[2][:, dt, cols_h], xs[2][:, dt, cols_h], xs[1][:, dt, cols_h], ALU.add
                                                ).then_inc(S["x2_ok"], 1)
                    else:
                        nc.vector.scalar_tensor_tensor(out=xs[2][:, dt, cols_h], in0=xs[2][:, dt, cols_h], scalar=1.0, in1=xs[1][:, dt, cols_h],
                                                       op0=ALU.mult, op1=ALU.add, accum_out=sum_a[:, 2, half:half + 1]
                                                       ).then_inc(S["ln2_sum"], 1)

            dve.wait_ge(S["mask_ok"], 1)
            for h in range(2):
                for dt in range(NT):
                    masked_source(h, dt)
                if h == 0:
                    dve.wait_ge(S["tu_pe"], 1)
                    nc.vector.tensor_copy(tu[:].rearrange("p t j h -> p t (j h)"),
                                          bank[TU][:, 0:NT * 2 * H].rearrange("p (t c) -> p t c", t=NT)).then_inc(S["tu_ok"], 1)
                    dve.wait_ge(S["tu_ok"], 1)
                    nc.vector.tensor_scalar(t4[:], tu[:, :, 0, :], STEEP, None, ALU.mult).then_inc(S["t4_ok"], 1)
                    nc.vector.tensor_scalar(nt[:], tu[:, 1, 0, :], -1.0, None, ALU.mult).then_inc(S["nt_ok"], 1)
                    dve.wait_ge(S["nt_ok"], 1)
                steep_side(h)
            largest_sums(0)
            masked_source(2, 0)
            largest_scores(0)
            masked_source(2, 1)
            shifts(0)
            steep_side(2)
            for dt in range(NT):
                masked_source(3, dt)
            steep_side(3)
            largest_sums(1)
            def sources_first(h):
                dve.wait_ge(S["termT_pe"], h + 1)
                nc.vector.tensor_copy(probs[:, h], halves(TB[h % len(TB)])).then_inc(S["probs_dve"], 1)

            for h in range(H):
                if HALF <= h + 2 < H:
                    steep_side(h + 2)
                two = 1 + h // 2 if h % 2 == 0 and h <= HALF else None
                times_counts(h, 0)
                if two is not None:
                    largest_scores(two)
                times_counts(h, 1)
                if two is not None:
                    shifts(two)
                if h < HALF:
                    for dt in range(NT):
                        masked_source(h + HALF, dt)
                    if h % 2:
                        largest_sums((h + HALF) // 2)
                if h - 1 in BY_DVE:
                    sources_first(h - 1)
                if h == 5:
                    weight_high(3)
            attention_out(0)
            attention_out(1)

            dve.wait_ge(S["x2_ok"], 2)
            layernorm_dve(2)
            split_h(2)
            for j in range(2):
                dve.wait_ge(S["h2T_hi"], j + 1)
                nc.vector.tensor_tensor(xT_part[1][:, 2 * j:2 * j + 2, :], halves(4 + j), xT_part[0][:, 2 * j:2 * j + 2, :].bitcast(F32),
                                        ALU.subtract).then_inc(S["h2T_lo"], 1)
            for j in range(2):
                dve.wait_ge(S["agg2_hi"], j + 1)
                nc.vector.tensor_tensor(agg2T_part[1][:, 2 * j:2 * j + 2, :], halves(j), agg2T_part[0][:, 2 * j:2 * j + 2, :].bitcast(F32),
                                        ALU.subtract).then_inc(S["agg2_lo"], 1)
            weight_high(4)

            def norm_features(m):
                dve.wait_ge(S["bnsd_ok"], m + 1)
                one = slice(m, m + 1)
                then(nc.vector.reciprocal(bn_rs[:, one], bn_sd[:, one]))
                then(nc.vector.tensor_tensor(bn_sc[:, one], bn_rs[:, one], cols_s[:, CGB + KT + m:CGB + KT + m + 1], ALU.mult))
                nc.vector.tensor_scalar(y_s[:, m, :], r_s[:, m, :], bn2[:, m, 0:1], bn_sc[:, one], ALU.subtract, ALU.mult
                                        ).then_inc(S["y_ok"], 1)

            for m in range(KT):
                dve.wait_ge(S["relu_ok"], m + 1)
                then(nc.vector.bn_stats(bn6[:, m, :], r_s[:, m, :]))
                nc.vector.bn_aggr(bn2[:, m, :], bn6[:, m, :]).then_inc(S["bn_ok"], 1)
                if m:
                    norm_features(m - 1)
            norm_features(KT - 1)

            dve.wait_ge(S["x2_beta"], NT)
            dve.wait_ge(S["yT_pe"], 1)
            nc.vector.scalar_tensor_tensor(out=xs[3][:, 0, :], in0=bank[0][:], scalar=1.0, in1=xs[2][:, 0, :], op0=ALU.mult, op1=ALU.add,
                                           accum_out=sum_a[:, 3, 0:1]).then_inc(S["ln3_sum"], 1)
            dve.wait_ge(S["yT_pe"], NT)
            then(nc.vector.tensor_tensor(xs[3][:, 1, :], bank[1][:], xs[2][:, 1, :], ALU.add))

            layernorm_dve(3, relu=False)
            split_h(3)
            dve.wait_ge(S["mat_hi"], 2)
            nc.vector.tensor_tensor(mat_part[1][:], halves(2), mat_part[0][:].bitcast(F32), ALU.subtract).then_inc(S["mat_lo"], 1)
            for j in range(2):
                dve.wait_ge(S["agg3_hi"], j + 1)
                nc.vector.tensor_tensor(xT_part[1][:, 2 * j:2 * j + 2, :], halves(4 + j), xT_part[0][:, 2 * j:2 * j + 2, :].bitcast(F32),
                                        ALU.subtract).then_inc(S["agg3_lo"], 1)
            for i, (t, a, b, out_bank) in enumerate(PIECES):
                dve.wait_ge(S["l3_pe"], i + 1)
                nc.vector.tensor_tensor(xs[4][:, t, a:b], bank[out_bank][:, a:b], xs[3][:, t, a:b], ALU.add).then_inc(S["x_ok"], 1)

        @block.tensor
        def _(pe):
            def project_1(t, a, b):
                for k in range(a, b):
                    for i, (x_part, part) in enumerate(THREE):
                        last = nc.tensor.matmul(bank[6 + t][:], xT_part[x_part][:, k, t * P:(t + 1) * P], w_part[part][:, k, :],
                                                start=(k + i == 0), stop=False)
                if b == KT:
                    for part in range(2):
                        last = nc.tensor.matmul(bank[6 + t][:], ones_r[:, 0:P], wb_part[part][:], start=False, stop=(part == 1))
                    last.then_inc(S["wx_pe"], 1)

            def keep_warm(b, n):
                pe.wait_ge(S["zeros_ok"], 1)
                for _ in range(n):
                    nc.tensor.matmul(bank[b][:], zeros[:, 0:P], zeros[:], start=True, stop=True)

            def count_edges(c):
                pe.wait_ge(S["hot_ok"], 2 * c + 2)
                for g in range(*CHUNKS[c]):
                    for i in range(2):
                        for half in range(NT):
                            last = nc.tensor.matmul(bank[half][:, 0:N], src_hot[:, g, half * P:(half + 1) * P, i],
                                                    dst_hot[:, g, :, i], start=(g + i == 0), stop=(g == PAIRS - 1 and i == 1))
                            if g == PAIRS - 1 and i == 1:
                                last.then_inc(S["counts_pe"], 1)
                            elif g == CHUNKS[c][1] - 1 and i == 1 and half == NT - 1:
                                last.then_inc(S["counted"], 1)

            def weigh_edges(a, b):
                for e in range(a, b):
                    for c, (first, _) in enumerate(CHUNKS):
                        if e == a and 2 * CHUNKS[c][1] > a and 2 * first <= a or e == 2 * first:
                            for part in range(3):
                                pe.wait_ge(S[f"srcw{part}_ok"], c + 1)
                    for half in range(NT):
                        for part in range(3):
                            last = nc.tensor.matmul(halves(2)[:, half, :], dst_hot[:, e // 2, half * P:(half + 1) * P, e % 2],
                                                    src_w[part][:, e // 2, :, e % 2], start=(e + half + part == 0),
                                                    stop=(e == ET - 1 and part == 2), skip_group_check=True)
                if b == ET:
                    last.then_inc(S["weighed_pe"], 1)

            def transpose_h(layer, name):
                for t in range(NT):
                    pe.wait_ge(S[f"ln{layer}_" + ("h_act", "h_dve")[t]], 1)
                    for k in range(KT):
                        last = nc.tensor.transpose(halves(4 + k // 2)[:, k % 2, t * P:(t + 1) * P],
                                                   hs[layer][:, t, k * P:(k + 1) * P], ident[:])
                        if t == NT - 1 and k % 2:
                            last.then_inc(S[name], 1)

            def project_0(t, a, b):
                for k in range(a, b):
                    for i, (x_part, part) in enumerate(THREE):
                        last = nc.tensor.matmul(bank[6 + t][:], xT_part[x_part][:, k, t * P:(t + 1) * P], w_part[part][:, k, :],
                                                start=(k + i == 0), stop=(k == KT - 1 and i == 2))
                if b == KT:
                    last.then_inc(S["hw_pe"], 1)

            def row_of(bank_ap, col_of):
                for t in range(NT):
                    last = nc.tensor.matmul(bank_ap[:, t * P:(t + 1) * P], col_of(t).broadcast_to([P, P]), ident[:], start=True, stop=True)
                return last

            def sym_times(mat, out_halves):
                for m in range(NT):
                    for k in range(NT):
                        last = nc.tensor.matmul(out_halves[:, m, :], sym[:, k, m * P:(m + 1) * P], mat[:, k, :], start=(k == 0), stop=(k == NT - 1))
                return last

            def aggregate_T(layer, banks, name):
                pe.wait_ge(S["mat_hi"], layer - 1)
                pe.wait_ge(S["h_hi0"], layer - 1)
                pe.wait_ge(S["h_hi1"], layer - 1)
                for j in range(2):
                    for i, (h, mat) in enumerate(((0, 0), (1, 0), (0, 1))):
                        if h:
                            pe.wait_ge(S["h_lo"], NT * (layer - 1))
                        if mat:
                            pe.wait_ge(S["mat_lo"], layer - 1)
                        for k in (2 * j, 2 * j + 1):
                            for t in range(NT):
                                last = nc.tensor.matmul(halves(banks[j])[:, k % 2, :], h_part[h][:, t, k * P:(k + 1) * P], mat_part[mat][:, t, :],
                                                        start=(i + k % 2 + t == 0), stop=(i == 2 and t == NT - 1), skip_group_check=True)
                    last.then_inc(S[name], 1)

            keep_warm(7, 6)
            count_edges(0)
            keep_warm(7, 3)
            count_edges(1)
            keep_warm(7, 5)
            count_edges(2)
            pe.wait_ge(S["ident_ok"], 1)
            transpose_h(0, "h0T_pe")
            count_edges(3)
            count_edges(4)
            weigh_edges(0, 1)
            pe.wait_ge(S["cnt_act"], NT)
            for a in range(NT):
                for b in range(NT):
                    last = nc.tensor.transpose(halves(3)[:, b, a * P:(a + 1) * P], cnt[:, a, b * P:(b + 1) * P], ident[:])
            last.then_inc(S["cntT_pe"], 1)
            pe.wait_ge(S["w0_lo"], 1)
            pe.wait_ge(S["h0T_lo"], 2)
            project_0(0, 0, KT)
            weigh_edges(1, 2)
            pe.wait_ge(S["poly0_ok"], NT)
            sym_times(poly[0], halves(4)).then_inc(S["prod1_pe"], 1)
            pe.wait_ge(S["rdeg_ok"], 1)
            row_of(bank[1], lambda t: rdeg[:, t:t + 1]).then_inc(S["rdegb_pe"], 1)
            project_0(1, 0, 2)
            pe.wait_ge(S["poly1_ok"], NT)
            sym_times(poly[1], halves(5)).then_inc(S["prod2_pe"], 1)
            project_0(1, 2, KT)
            pe.wait_ge(S["poly2_ok"], NT)
            for t in range(NT):
                for k in range(NT):
                    if t == 0:
                        pe.wait_ge(S["hwb_ok"], k + 1)
                    last = nc.tensor.matmul(bank[MIX + t][:], poly[2][:, k, t * P:(t + 1) * P], hwb[:, k, :], start=(k == 0), stop=(k == NT - 1))
                last.then_inc(S["mix_pe"], 1)

            weigh_edges(2, 8)

            transpose_h(1, "h1T_pe")
            weigh_edges(8, 10)
            pe.wait_ge(S["v_hi"], 1)
            for i, (x_part, part) in enumerate(THREE):
                if i == 1:
                    pe.wait_ge(S["v_lo"], 1)
                for k in range(KT):
                    if part == 0 and k % 2 == 0:
                        pe.wait_ge(S[("h1T_hi", "h1T_lo")[x_part]], k // 2 + 1)
                    nc.tensor.matmul(bank[3][0:2 * H, 0:N], v_part[part][:, k], xT_part[x_part][:, k, :], start=(k + i == 0), stop=False)
            pe.wait_ge(S["ones_ok"], 1)
            for part in range(2):
                last = nc.tensor.matmul(bank[3][0:2 * H, 0:N], v_part[part][0:1, KT], ones_r[:], start=False, stop=(part == 1))
            last.then_inc(S["tuT_pe"], 1)
            pe.wait_ge(S["ws_hi"], 1)
            pe.wait_ge(S["ws_lo"], 1)
            project_1(0, 0, 2)
            pe.wait_ge(S["tuT_lo"], 1)
            pe.wait_ge(S["identr_ok"], 1)

            def source_rows(g):
                for r in range(2):
                    row = H + 2 * g + r
                    for part in range(2):
                        last = nc.tensor.matmul(halves(UB[g])[:, r, :], ident_r[:, row:row + 1].broadcast_to([16, P]), tuT[part][:],
                                                start=(part == 0), stop=(part == 1))
                last.then_inc(S["ub_pe"], 1)

            source_rows(0)
            for t in range(NT):
                for part in range(2):
                    last = nc.tensor.matmul(bank[TU][:, 2 * H * t:2 * H * (t + 1)], tuT[part][:, t * P:(t + 1) * P], ident_r[:],
                                            start=(part == 0), stop=(part == 1))
            last.then_inc(S["tu_pe"], 1)
            source_rows(1)
            pe.wait_ge(S["cntmean_ok"], 1)
            source_rows(2)
            pe.wait_ge(S["tu_ok"], 1)
            source_rows(3)

            def wait_probs(h):
                if h in BY_DVE:
                    pe.wait_ge(S["probs_dve"], sum(i <= h for i in BY_DVE))
                else:
                    pe.wait_ge(S["probs_act"], sum(i <= h for i in range(H) if i not in BY_DVE))

            def transpose_terms(h):
                pe.wait_ge(S["term_ok"], NT * h + NT)
                if h >= len(TB):
                    wait_probs(h - len(TB))
                elif h:
                    pe.wait_ge(S["wx_ok"], h)
                for dt in range(NT):
                    for st in range(NT):
                        last = nc.tensor.transpose(halves(TB[h % len(TB)])[:, st, dt * P:(dt + 1) * P], term[h % ZB][:, dt, st * P:(st + 1) * P],
                                                   ident[:])
                last.then_inc(S["termT_pe"], 1)

            def attend(h):
                wait_probs(h)
                if h == HALF:
                    pe.wait_ge(S["zmax_ok"], NT * H)
                for dt in range(NT):
                    for st in range(NT):
                        last = nc.tensor.matmul(bank[ATT[h // HALF][dt]][:, h * DP:(h + 1) * DP], probs[:, h, st, dt * P:(dt + 1) * P],
                                                wx[:, st, h, :], start=(st == 0), stop=(st == NT - 1))
                    if h % HALF == HALF - 1:
                        last.then_inc(S["att_pe"], 1)

            pe.wait_ge(S["wb_lo"], 1)
            project_1(0, 2, KT)
            project_1(1, 0, KT)
            transpose_terms(0)
            weigh_edges(10, 12)
            pe.wait_ge(S["wx_ok"], NT)
            pe.wait_ge(S["zmax_ok"], NT * HALF)
            for h in range(H):
                if h + 1 < H:
                    transpose_terms(h + 1)
                attend(h)
                if h < HALF:
                    weigh_edges(12 + h, 13 + h)

            weigh_edges(16, 22)
            transpose_h(2, "h2T_pe")
            weigh_edges(22, 23)
            aggregate_T(2, (0, 1), "agg2_pe")
            pe.wait_ge(S["h2T_hi"], 2)
            pe.wait_ge(S["h2T_lo"], 2)
            pe.wait_ge(S["wr_hi"], KT)
            pe.wait_ge(S["wr_lo"], 1)
            for m in range(KT):
                for k in range(KT):
                    for i, (x_part, part) in enumerate(THREE):
                        last = nc.tensor.matmul(bank[4 + m][:, 0:N], w_part[part][:, k, m * P:(m + 1) * P], xT_part[x_part][:, k, :],
                                                start=(k + i == 0), stop=False)
            last.then_inc(S["l2r_pe"], 1)
            pe.wait_ge(S["agg2_lo"], 2)
            pe.wait_ge(S["wl_lo"], 1)
            for m in range(KT):
                for k in range(KT):
                    for i, (x_part, part) in enumerate(THREE):
                        last = nc.tensor.matmul(bank[4 + m][:, 0:N], wl_part[part][:, k, m * P:(m + 1) * P], agg2T_part[x_part][:, k, :],
                                                start=False, stop=(k == KT - 1 and i == 2))
                last.then_inc(S["l2_pe"], 1)
            weigh_edges(23, 27)
            for m in range(KT):
                pe.wait_ge(S["y_ok"], m + 1)
                for t in range(NT):
                    last = nc.tensor.transpose(bank[t][:, m * P:(m + 1) * P], y_s[:, m, t * P:(t + 1) * P], ident[:])
                    if m == KT - 1:
                        last.then_inc(S["yT_pe"], 1)

            weigh_edges(27, ET)
            keep_warm(3, 1)
            
            aggregate_T(3, (4, 5), "agg3_pe")
            pe.wait_ge(S["w3_hi"], 1)
            pe.wait_ge(S["w3_lo"], 1)

            def project_3(piece, k_half):
                t, a, b, out_bank = PIECES[piece]
                for i, (x_part, part) in enumerate(THREE):
                    pe.wait_ge(S[("agg3_hi", "agg3_lo")[x_part]], k_half + 1)
                    for k in range(2 * k_half, 2 * k_half + 2):
                        last = nc.tensor.matmul(bank[out_bank][:, a:b], xT_part[x_part][:, k, t * P:(t + 1) * P], w_part[part][:, k, a:b],
                                                start=(k + i == 0), stop=(k == KT - 1 and i == 2))
                if k_half == 1:
                    last.then_inc(S["l3_pe"], 1)

            for piece, k_half in ((0, 0), (1, 0), (0, 1), (1, 1), (2, 0), (2, 1)):
                project_3(piece, k_half)


def kernel(x, src, dst, edge_weight, L0_gnn_W, L0_gnn_b, L0_gnn_diffusion_weights, L1_gnn_Ws, L1_gnn_Wb, L1_gnn_a_w,
           L1_gnn_a_b, L2_gnn_W_l, L2_gnn_b_l, L2_gnn_W_r, L2_gnn_gamma, L2_gnn_beta, L3_gnn_weight):
    import numpy as np
    import concourse.bacc as bacc
    from concourse.bass_utils import run_bass_kernel_spmd

    def a(v):
        return np.asarray(v)

    p, d = 128, x.shape[1]
    ws = a(L1_gnn_Ws)
    heads = ws.shape[0]
    dp = ws.shape[2]
    cols = np.concatenate([a(L2_gnn_b_l).reshape(d // p, p).T, a(L2_gnn_gamma).reshape(d // p, p).T], axis=1)
    rows = np.concatenate([a(L0_gnn_b), a(L1_gnn_Wb).reshape(-1), a(L0_gnn_diffusion_weights), a(L1_gnn_a_b),
                           a(L2_gnn_beta), a(L1_gnn_a_w).reshape(heads, 2, dp).transpose(1, 0, 2).reshape(-1)])[None, :]
    arrays = {
        "x": a(x),
        "edges": np.stack([a(src).reshape(p, -1), a(dst).reshape(p, -1)], axis=1),
        "edge_w": a(edge_weight).reshape(p, -1),
        "w0": a(L0_gnn_W),
        "ws": ws.transpose(1, 0, 2).reshape(d, heads * dp),
        "wl_T": a(L2_gnn_W_l).T, "wr_T": a(L2_gnn_W_r).T, "w3_T": a(L3_gnn_weight).T,
        "rows": rows, "cols": cols,
    }
    arrays = {f"in_{k}": np.ascontiguousarray(v) for k, v in arrays.items()}
    nc = bacc.Bacc("TRN2", target_bir_lowering=False, num_devices=1)
    ins = [nc.dram_tensor(k, v.shape, mybir.dt.from_np(v.dtype), kind="ExternalInput").ap() for k, v in arrays.items()]
    out = nc.dram_tensor("out", x.shape, F32, kind="ExternalOutput").ap()
    gnn_program(nc, *ins, out)
    done = run_bass_kernel_spmd(nc, [arrays], core_ids=[0])
    return done.results[0]["out"]
```
